# Optimizing a Trainium2 kernel written in Bass

```python
import numpy as np
import jax
import jax.numpy as jnp

def _softmax(x, axis=-1):
    return jax.nn.softmax(x, axis=axis)

def _gelu(x):
    return jax.nn.gelu(x, approximate=True)

def _silu(x):
    return jax.nn.silu(x)

def _sigmoid(x):
    return jax.nn.sigmoid(x)

def _layernorm(x, axis=-1, eps=1e-05):
    m = jnp.mean(x, axis=axis, keepdims=True)
    v = jnp.var(x, axis=axis, keepdims=True)
    return (x - m) / jnp.sqrt(v + eps)

def _scatter_add(tgt, idx, src, axis=0):
    return tgt.at[idx].add(src)

def _segment_sum(src, seg, n):
    return jax.ops.segment_sum(src, seg, n)
kernel_name = 'mk_gps_d1_gnn_r8_f449ae'

def setup_inputs(seed: int=0):
    np.random.seed(seed)
    _w = jnp.asarray

    def _rec_inputs():
        import jax
        import jax.numpy as jnp
        _gk = jax.random.key(seed)
        x = -6.415e-05 + 1 * jax.random.normal(jax.random.fold_in(_gk, 1), (1250, 512), jnp.float32)
        src = jax.random.randint(jax.random.fold_in(_gk, 2), (40000,), 0, 1250, jnp.int32)
        dst = jnp.minimum((1250 * jax.random.uniform(jax.random.fold_in(_gk, 3), (40000,)) ** 2.0).astype(jnp.int32), 9999)
        _o = jnp.argsort(dst, stable=True)
        src = src[_o]
        dst = dst[_o]
        edge_type_8 = jax.random.randint(jax.random.fold_in(_gk, 12), (40000,), 0, 8, jnp.int32)
        return (x, src, dst, edge_type_8)
    x, src, dst, edge_type_8 = _rec_inputs()

    def _L0_gnn_setup():
        import jax, jax.numpy as jnp
        import numpy as np
        N_NODES = 2500
        N_EDGES = 40000
        N_REL = 8
        D_IN = 512
        D_OUT = 512
        key = jax.random.key(seed)
        k1, k2, k3, k4, k5 = jax.random.split(key, 5)
        x = jax.random.normal(k1, (N_NODES, D_IN), dtype=jnp.float32)
        W_self = jax.random.normal(k2, (D_OUT, D_IN), dtype=jnp.float32) * 0.05
        W_rel = jax.random.normal(k3, (N_REL, D_OUT, D_IN), dtype=jnp.float32) * 0.05
        bias = jnp.zeros((D_OUT,), dtype=jnp.float32)
        edge_index = jax.random.randint(k4, (2, N_EDGES), 0, N_NODES, dtype=jnp.int64)
        edge_type = jax.random.randint(k5, (N_EDGES,), 0, N_REL, dtype=jnp.int64)
        return {'x': x, 'W_self': W_self, 'W_rel': W_rel, 'bias': bias, 'edge_index': edge_index, 'edge_type': edge_type}
    _L0_gnn_all = _L0_gnn_setup()
    _L0_gnn_in = {k: v for k, v in _L0_gnn_all.items() if k in ('W_self', 'W_rel', 'bias')}
    del _L0_gnn_all

    def _L0_mix_setup():
        import jax, jax.numpy as jnp
        import numpy as np
        B, N, DIM = (4, 256, 512)
        H, HD = (8, 64)
        SCALE = 1.0 / float(np.sqrt(HD))
        key = jax.random.key(seed)
        k1, k2, k3 = jax.random.split(key, 3)
        x = jax.random.normal(k1, (B, N, DIM), dtype=jnp.float32)
        w_qkv = jax.random.normal(k2, (DIM, 3 * H * HD), dtype=jnp.float32) * 0.02
        w_out = jax.random.normal(k3, (H * HD, DIM), dtype=jnp.float32) * 0.02
        b_out = jnp.zeros((DIM,), dtype=jnp.float32)
        return {'x': x, 'w_qkv': w_qkv, 'w_out': w_out, 'b_out': b_out}
    _L0_mix_all = _L0_mix_setup()
    _L0_mix_in = {k: v for k, v in _L0_mix_all.items() if k in ('w_qkv', 'w_out', 'b_out')}
    del _L0_mix_all

    def _L0_ffn_setup():
        import jax, jax.numpy as jnp
        import numpy as np
        B, S, H, E, K = (8, 512, 512, 8, 2)
        key = jax.random.key(seed)
        ks = jax.random.split(key, 7)
        s_h = 1.0 / np.sqrt(H)
        s_2h = 1.0 / np.sqrt(2 * H)
        return {'x': jax.random.normal(ks[0], (B, S, H), dtype=jnp.float32), 'gate_w': jax.random.uniform(ks[1], (H, E), minval=-s_h, maxval=s_h, dtype=jnp.float32), 'gate_b': jax.random.uniform(ks[2], (E,), minval=-s_h, maxval=s_h, dtype=jnp.float32), 'w1': jax.random.uniform(ks[3], (E, H, 2 * H), minval=-s_h, maxval=s_h, dtype=jnp.float32), 'b1': jax.random.uniform(ks[4], (E, 2 * H), minval=-s_h, maxval=s_h, dtype=jnp.float32), 'w2': jax.random.uniform(ks[5], (E, 2 * H, H), minval=-s_2h, maxval=s_2h, dtype=jnp.float32), 'b2': jax.random.uniform(ks[6], (E, H), minval=-s_2h, maxval=s_2h, dtype=jnp.float32)}
    _L0_ffn_all = _L0_ffn_setup()
    _L0_ffn_in = {k: v for k, v in _L0_ffn_all.items() if k in ('gate_w', 'gate_b', 'w1', 'b1', 'w2', 'b2')}
    del _L0_ffn_all
    return {'x': x, 'src': src, 'dst': dst, 'edge_type_8': edge_type_8, 'L0_gnn_W_self': _L0_gnn_in['W_self'], 'L0_gnn_W_rel': _L0_gnn_in['W_rel'], 'L0_gnn_bias': _L0_gnn_in['bias'], 'L0_mix_w_qkv': _L0_mix_in['w_qkv'], 'L0_mix_w_out': _L0_mix_in['w_out'], 'L0_mix_b_out': _L0_mix_in['b_out'], 'L0_ffn_gate_w': _L0_ffn_in['gate_w'], 'L0_ffn_gate_b': _L0_ffn_in['gate_b'], 'L0_ffn_w1': _L0_ffn_in['w1'], 'L0_ffn_b1': _L0_ffn_in['b1'], 'L0_ffn_w2': _L0_ffn_in['w2'], 'L0_ffn_b2': _L0_ffn_in['b2']}

def reference(x, src, dst, edge_type_8, L0_gnn_W_self, L0_gnn_W_rel, L0_gnn_bias, L0_mix_w_qkv, L0_mix_w_out, L0_mix_b_out, L0_ffn_gate_w, L0_ffn_gate_b, L0_ffn_w1, L0_ffn_b1, L0_ffn_w2, L0_ffn_b2):
    import jax
    import jax.numpy as jnp

    def _L0_gnn_ref(x, W_self, W_rel, bias, edge_index, edge_type):
        import jax, jax.numpy as jnp
        import numpy as np
        N_NODES = 2500
        N_EDGES = 40000
        N_REL = 8
        D_IN = 512
        D_OUT = 512
        N = x.shape[0]
        R, d_out, _ = W_rel.shape
        src, dst = (edge_index[0], edge_index[1])
        out = jnp.einsum('ni,oi->no', x, W_self)
        h_rel = jnp.einsum('ni,roi->rno', x, W_rel)
        msg = h_rel[edge_type, src]
        seg = edge_type * N + dst
        agg = jax.ops.segment_sum(msg, seg, num_segments=R * N).reshape(R, N, d_out)
        cnt = jax.ops.segment_sum(jnp.ones((msg.shape[0],), dtype=x.dtype), seg, num_segments=R * N).reshape(R, N, 1)
        cnt = jnp.maximum(cnt, 1.0)
        out = out + jnp.sum(agg / cnt, axis=0)
        return out + bias

    def _L0_mix_ref(x, w_qkv, w_out, b_out):
        import jax, jax.numpy as jnp
        import numpy as np
        B, N, DIM = (4, 256, 512)
        H, HD = (8, 64)
        SCALE = 1.0 / float(np.sqrt(HD))
        b, n, c = x.shape
        qkv = x @ w_qkv
        qkv = qkv.reshape(b, n, 3, H, HD)
        q = qkv[:, :, 0].transpose(0, 2, 1, 3)
        k = qkv[:, :, 1].transpose(0, 2, 1, 3)
        v = qkv[:, :, 2].transpose(0, 2, 1, 3)
        attn = jnp.einsum('bhnd,bhmd->bhnm', q, k) * (SCALE / n)
        out = jnp.einsum('bhnm,bhmd->bhnd', attn, v)
        out = out.transpose(0, 2, 1, 3).reshape(b, n, H * HD)
        return out @ w_out + b_out

    def _L0_ffn_ref(x, gate_w, gate_b, w1, b1, w2, b2):
        import jax, jax.numpy as jnp
        import numpy as np
        B, S, H, E, K = (8, 512, 512, 8, 2)
        logits = jnp.einsum('bsh,he->bse', x, gate_w) + gate_b
        topk_vals, topk_idx = jax.lax.top_k(logits, K)
        topk_weights = jax.nn.softmax(topk_vals, axis=-1)
        mask = jax.nn.one_hot(topk_idx, E, dtype=topk_weights.dtype)
        weights = jnp.einsum('bske,bsk->bse', mask, topk_weights)
        h = jax.nn.relu(jnp.einsum('bsh,ehf->bsef', x, w1) + b1)
        expert_out = jnp.einsum('bsef,efh->bseh', h, w2) + b2
        return jnp.einsum('bseh,bse->bsh', expert_out, weights)
    edge_index = jnp.stack([src, dst])
    xn = _layernorm(x, axis=-1)
    x = x + _L0_gnn_ref(xn, L0_gnn_W_self, L0_gnn_W_rel, L0_gnn_bias, edge_index, edge_type_8) + _L0_mix_ref(xn[None], L0_mix_w_qkv, L0_mix_w_out, L0_mix_b_out)[0]
    x = x + _L0_ffn_ref(_layernorm(x, axis=-1)[None], L0_ffn_gate_w, L0_ffn_gate_b, L0_ffn_w1, L0_ffn_b1, L0_ffn_w2, L0_ffn_b2)[0]
    return x

_drawn_inputs = setup_inputs


def setup_inputs(seed=0):
    import zlib

    import numpy as np

    out = dict(_drawn_inputs(seed))
    spreads = {'L0_gnn_bias': (0.0, 0.732), 'L0_mix_b_out': (0.0, 0.734)}
    factors = {'L0_mix_w_qkv': 8.0,
     'L0_mix_w_out': 8.0,
     'L0_ffn_gate_b': 34.825,
     'L0_ffn_b1': 64.0,
     'L0_ffn_b2': 40.571,
     'L0_ffn_gate_w': 2.91,
     'L0_ffn_w1': 3.685,
     'L0_ffn_w2': 2.902}
    for name, (base, spread) in spreads.items():
        noise = np.random.default_rng([zlib.crc32(name.encode()), seed]).standard_normal(out[name].shape)
        drawn = base * np.exp(spread * noise) if base else spread * noise
        out[name] = jnp.asarray(drawn.astype(out[name].dtype))
    for name, factor in factors.items():
        out[name] = (out[name] * factor).astype(out[name].dtype)
    return out
```

```python
from contextlib import ExitStack

import concourse.bass as bass
from concourse import mybir

ALU = mybir.AluOpType
ACT = mybir.ActivationFunctionType
AX_X = mybir.AxisListType.X
F32 = mybir.dt.float32
F16 = mybir.dt.float16
BF16 = mybir.dt.bfloat16
I32 = mybir.dt.int32

P = 128


def gnn_moe_kernel(nc, x, src, dst, etype, w_self_t, w_rel_t, gnn_bias, w_q_t, w_k, w_v, w_out, b_out,
                   gate_w, gate_b, w1, b1_cols, w2, b2, out):
    N, D = x.shape
    KD = D // P
    NT = (N + P - 1) // P
    TAIL = N - (NT - 1) * P
    NPAD = NT * P
    R = w_rel_t.shape[0]
    E = src.shape[0]
    EJ = E // P
    ETAIL = E - EJ * P
    EC = EJ + (ETAIL > 0)
    NB = NT * R
    HALF = 7
    GRP = 2 * HALF
    TILES = -(-((E + NB * (P - 1)) // P) // GRP) * GRP
    NX = w1.shape[0]
    F = w1.shape[2]
    KF = F // P
    TOPK = 2
    XT_TILES = (TOPK * N + NX * (P - 1)) // P
    EPS = 1e-5
    HEAD = 64
    MIX_SCALE = (1.0 / float(HEAD) ** 0.5) / N
    SORT = 5
    NO_TILE = float(P * 500)
    assert XT_TILES % 2 == 1 and EC - (R // 2 - 1) * 2 * SORT * NT < 20 and TILES <= 512

    h_table = nc.dram_tensor("h_table", [R * NPAD, D], F32).ap()
    x_slots = nc.dram_tensor("x_slots", [XT_TILES * P, D], F32).ap()
    y_slots = nc.dram_tensor("y_slots", [XT_TILES * P, D], F32).ap()

    with ExitStack() as ctx:
        def sb(name, shape, dt=F32):
            return ctx.enter_context(nc.sbuf_tensor(name, shape, dt))

        def sem(name):
            return ctx.enter_context(nc.semaphore(name))

        x2 = sb("x2", [P, NT, D])
        xn = sb("xn", [P, NT, D])
        xnT = sb("xnT", [P, KD, NPAD])
        wrel = sb("wrel", [P, 2, KD, D])
        arena = sb("arena", [P, 8, KD * D])
        wk_sb, wv_sb, wqT_sb, wout_sb, wself_sb, gram, u_sb, tt_sb = (
            arena[:, n, :].rearrange("p (k d) -> p k d", k=KD) for n in range(8))
        wtot = gram
        mbd = sb("mbd", [P, KD, P])
        stage = sb("stage", [P, 4, D])
        src_i = sb("src_i", [P, EC], I32)
        dst_i = sb("dst_i", [P, EC], I32)
        typ_i = sb("typ_i", [P, EC], I32)
        tmp_i = sb("tmp_i", [P, EC], I32)
        src_f = sb("src_f", [P, EC])
        dloc_f = sb("dloc_f", [P, EC])
        code_f = sb("code_f", [P, EC])
        bkt_f = sb("bkt_f", [P, EC])
        bkt_h = sb("bkt_h", [P, EC], BF16)
        zeros_h = sb("zeros_h", [P, EC], BF16)
        slot_f = sb("slot_f", [P, EC])
        slot_i = src_i
        row_f = dst_i[:].bitcast(F32)
        tile_f = typ_i[:].bitcast(F32)
        tot = sb("tot", [P, NB])
        cols = sb("cols", [P, 6, NB])
        cols_i = sb("cols_i", [P, 2, NB], I32)
        rank_from = sb("rank_from", [P, NB])
        inv_cnt = sb("inv_cnt", [P, NB])
        tilecol = sb("tilecol", [P, 4])
        bt_col = sb("bt_col", [P, 4])
        bt_i = sb("bt_i", [1, 2, 4 * P], I32)
        widths = [P, P, NB, TILES, TILES]
        work = sb("work", [P, max(SORT * sum(widths) // 2, HALF * D + GRP * P)])
        half = work[:, 0:SORT * sum(widths) // 2].bitcast(F16)
        oh_row, oh_loc, oh_bkt, oh_src, oh_code = (
            half[:, SORT * sum(widths[:n]):SORT * sum(widths[:n + 1])].rearrange("p (s n) -> p s n", s=SORT)
            for n in range(5))
        bias_row = work[:, 0:2 * D].rearrange("p (s d) -> p s d", s=2)
        rank_f = work[:, 2 * D:2 * D + 2 * EC].rearrange("p (s j) -> p s j", s=2)
        eq_h = work[:, 4 * D:4 * D + EC].bitcast(BF16).rearrange("p (s j) -> p s j", s=2)
        bt_junk = work[:, 5 * D:5 * D + 4 * NB].rearrange("p (m b) -> p m b", m=4)
        msg = work[:, 0:HALF * D].rearrange("p (s d) -> p s d", s=HALF)
        oh_dst = work[:, HALF * D:HALF * D + GRP * P].rearrange("p (s n) -> p s n", s=GRP)
        iota_h = sb("iota_h", [P, TILES], F16)
        iota_f = sb("iota_f", [P, P + 1])
        dist = sb("dist", [P, 2, P])
        diff = sb("diff", [P, P])
        ident = sb("ident", [P, P])
        below = sb("below", [P, P])
        ones = sb("ones", [P, P])
        code_i = arena[:, 1, 0:TILES].bitcast(I32)
        part_i = arena[:, 1, TILES:3 * TILES].bitcast(I32).rearrange("p (a t) -> p a t", a=2)
        gidx = sb("gidx", [P, TILES], I32)
        ndst = sb("ndst", [P, TILES])
        idx_ring = sb("idx_ring", [P, 2, HALF], I32)
        stats = sb("stats", [P, NT, 6])
        mv = sb("mv", [P, NT, 2])
        vare = sb("vare", [P, NT])
        std = sb("std", [P, NT])
        rstd = sb("rstd", [P, NT])
        zrow = mbd[:].rearrange("p k m -> p (k m)")
        gate_sb = sb("gate_sb", [P, KD, NX])
        gb_row = sb("gb_row", [P, NX])
        b1_sb = sb("b1_sb", [P, NX * KF])
        b2_sb = sb("b2_sb", [NX, D])
        logit = sb("logit", [P, NT, NX])
        masked = sb("masked", [P, NT, NX])
        pick = sb("pick", [P, 2, NT, NX])
        score = sb("score", [P, NT, NX])
        order = sb("order", [P, NT, NX])
        valid = sb("valid", [P, NT, NX])
        top = sb("top", [P, 2, NT])
        best = sb("best", [P, NT])
        wexp = sb("wexp", [P, 3, NT])
        wts = sb("wts", [P, 2, NT])
        wfull = sb("wfull", [P, NT, NX])
        wpart = sb("wpart", [P, NT, NX])
        took = sb("took", [P, NX, NT])
        tsum = sb("tsum", [P, NX, NT])
        tcum = sb("tcum", [P, NX, NT])
        xslot = sb("xslot", [P, NX, NT])
        xcols = sb("xcols", [P, 6, NX])
        xcols_i = sb("xcols_i", [P, NX], I32)
        pick_slot = sb("pick_slot", [P, NT, NX])
        slots_f = sb("slots_f", [P, 2, NT])
        slots_i = sb("slots_i", [P, 2, NT], I32)
        et_col = sb("et_col", [P, 1])
        et_junk = sb("et_junk", [P, NX])
        et_i = sb("et_i", [1, P], I32)
        wT = dist[0:NX]

        bank = [ctx.enter_context(nc.psum_tensor(f"bank{n}", [P, 512], F32)) for n in range(8)]

        x_in = sem("x_in")
        x_tail_in = sem("x_tail_in")
        edges_in = sem("edges_in")
        wrel_in = [sem("wrel_in0"), sem("wrel_in1")]
        mix_in = sem("mix_in")
        small_in = sem("small_in")
        edge_memset = sem("edge_memset")
        x_memset = sem("x_memset")
        consts = sem("consts")
        pool_step = sem("pool_step")
        dve_step = sem("dve_step")
        std_ready = sem("std_ready")
        var_ready = sem("var_ready")
        xn_ready = sem("xn_ready")
        tr_done = sem("tr_done")
        tr_copied = sem("tr_copied")
        h_done = sem("h_done")
        h_copied = sem("h_copied")
        h_stored = [sem(f"h_stored{n}") for n in range(4)]
        tot_ready = sem("tot_ready")
        off_done = sem("off_done")
        mix_done = sem("mix_done")
        mix_copied = sem("mix_copied")
        wtot_ready = sem("wtot_ready")
        base_done = sem("base_done")
        base_added = sem("base_added")
        rank1 = sem("rank1")
        rank2 = sem("rank2")
        slots_set = sem("slots_set")
        copy_turn = sem("copy_turn")
        oh_ready = sem("oh_ready")
        oh_used = sem("oh_used")
        bt_ready = sem("bt_ready")
        bt_done = sem("bt_done")
        gidx_ready = sem("gidx_ready")
        idx_copied = sem("idx_copied")
        gather_turn = sem("gather_turn")
        gathered = [sem(f"gathered{n}") for n in range(HALF)]
        ndst_ready = sem("ndst_ready")
        dist_ready = sem("dist_ready")
        ohd_ready = sem("ohd_ready")
        agg_done = sem("agg_done")
        agg_added = sem("agg_added")
        logit_done = sem("logit_done")
        gap_ready = sem("gap_ready")
        exp_ready = sem("exp_ready")
        took_ready = sem("took_ready")
        cum_done = sem("cum_done")
        slots_ready = sem("slots_ready")
        et_ready = sem("et_ready")
        et_done = sem("et_done")
        et_int = sem("et_int")
        x_zeroed = sem("x_zeroed")
        x_scattered = sem("x_scattered")
        wfull_ready = sem("wfull_ready")
        wT_done = sem("wT_done")
        wT_copied = sem("wT_copied")
        b2_done = sem("b2_done")
        b2_added = sem("b2_added")
        w1_in = [sem("w1_in0"), sem("w1_in1")]
        w2_in = [sem("w2_in0"), sem("w2_in1")]
        xs_in = [sem("xs_in0"), sem("xs_in1")]
        xT_done = sem("xT_done")
        xT_copied = sem("xT_copied")
        l1_done = sem("l1_done")
        l1_copied = sem("l1_copied")
        l2_done = sem("l2_done")
        y_copied = sem("y_copied")
        y_stored = [sem("y_stored0"), sem("y_stored1")]
        y_back = [sem(f"y_back{n}") for n in range(4)]
        out_ready = sem("out_ready")
        out_stored = sem("out_stored")

        ew1 = [arena[:, 4 * b:4 * b + 2, :].rearrange("p a n -> p (a n)").rearrange("p (k f) -> p k f", k=KD)
               for b in range(2)]
        ew2 = [arena[:, 4 * b + 2:4 * b + 4, :].rearrange("p a n -> p (a n)").rearrange("p (k d) -> p k d", k=KF)
               for b in range(2)]
        xs = wrel[:, 0, 0:2, :]
        xsT = wrel[:, 0, 2:4, :].rearrange("p a (k m) -> p a k m", k=KD)
        hT = wrel[:, 1, 0:2, :].rearrange("p a (k m) -> p (a k) m", m=P)
        y_sb = wrel[:, 1, 2:4, :]
        y_ring = msg[:, 0:4, :]

        block = ctx.enter_context(nc.Block())

        def at_least(eng, s, value):
            if not (isinstance(value, int) and value <= 0):
                eng.wait_ge(s, value)

        @block.sync
        def _(sp):
            sp.dma_start(src_i[:, 0:EJ], src[0:EJ * P].rearrange("(p j) -> p j", p=P)).then_inc(edges_in, 16)
            sp.dma_start(dst_i[:, 0:EJ], dst[0:EJ * P].rearrange("(p j) -> p j", p=P)).then_inc(edges_in, 16)
            sp.dma_start(typ_i[:, 0:EJ], etype[0:EJ * P].rearrange("(p j) -> p j", p=P)).then_inc(edges_in, 16)
            sp.dma_start(x2[:, 0:NT - 1, :], x[0:(NT - 1) * P, :].rearrange("(t p) d -> p t d", p=P)).then_inc(x_in, 16)
            sp.wait_ge(x_memset, 1)
            sp.dma_start(x2[0:TAIL, NT - 1, :], x[(NT - 1) * P:N, :]).then_inc(x_tail_in, 16)
            sp.wait_ge(edge_memset, 3)
            for t_sb, t_dram in ((src_i, src), (dst_i, dst), (typ_i, etype)):
                sp.dma_start(t_sb[0:ETAIL, EJ:EC], t_dram[EJ * P:E].rearrange("(p j) -> p j", j=1)).then_inc(edges_in, 16)
            for b in range(2):
                sp.dma_start(wrel[:, b], w_rel_t[b].rearrange("(k p) o -> p k o", p=P)).then_inc(wrel_in[b], 16)
            for t_sb, t_dram in ((wk_sb, w_k), (wv_sb, w_v), (wqT_sb, w_q_t), (wout_sb, w_out), (wself_sb, w_self_t)):
                sp.dma_start(t_sb, t_dram.rearrange("(k p) o -> p k o", p=P)).then_inc(mix_in, 16)
            sp.dma_start(bias_row[:, 0, :], gnn_bias.partition_broadcast(P)).then_inc(small_in, 16)
            sp.dma_start(bias_row[:, 1, :], b_out.partition_broadcast(P)).then_inc(small_in, 16)
            sp.dma_start(gb_row[:], gate_b.partition_broadcast(P)).then_inc(small_in, 16)
            sp.dma_start(gate_sb[:], gate_w.rearrange("(k p) e -> p k e", p=P)).then_inc(small_in, 16)
            sp.dma_start(b1_sb[:], b1_cols).then_inc(small_in, 16)
            sp.dma_start(b2_sb[:], b2).then_inc(small_in, 16)

            def load_type(i, h):
                sp.wait_ge(h_done, ((i - 1) * 2 + h + 1) * NT)
                sp.dma_start(wrel[:, h],
                             w_rel_t[bass.ds(i * 2 + h, 1), :, :].rearrange("a (k p) o -> p (a k) o", p=P)
                             ).then_inc(wrel_in[h], 16)

            def types(i, last):
                for h in range(2):
                    for t in range(NT):
                        g = i * 2 * NT + h * NT + t
                        sp.wait_ge(h_copied, g + 1)
                        sp.dma_start(h_table[bass.ds((i * 2 + h) * NPAD + t * P, P), :],
                                     stage[:, (h * NT + t) % 4, :]).then_inc(h_stored[(h * NT + t) % 4], 16)
                    if not last:
                        load_type(i + 1, h)

            types(0, False)
            with sp.Fori(1, R // 2 - 1) as i:
                types(i, False)
            types(R // 2 - 1, True)

            sp.wait_ge(et_int, 1)
            sp.wait_ge(x_zeroed, 16)
            sp.wait_ge(base_added, NT)

            def expert_load(s, b, first):
                e = sp.value_load(et_i[0:1, bass.ds(s, 1)], min_val=0, max_val=NX - 1)
                if not first:
                    sp.wait_ge(l1_done, (s - 1) * KF)
                sp.dma_start(ew1[b], w1[bass.ds(e, 1), :, :].rearrange("a (k p) f -> p (a k) f", p=P)).then_inc(w1_in[b], 16)
                if not first:
                    sp.wait_ge(l2_done, s - 1)
                sp.dma_start(ew2[b], w2[bass.ds(e, 1), :, :].rearrange("a (k p) d -> p (a k) d", p=P)).then_inc(w2_in[b], 16)
                if first:
                    sp.wait_ge(x_scattered, 16 * 2 * NT)
                else:
                    sp.wait_ge(xT_done, s - 1)
                sp.dma_start(xs[:, b, :], x_slots[bass.ds(s * P, P), :]).then_inc(xs_in[b], 16)

            expert_load(0, 0, True)
            expert_load(1, 1, True)
            with sp.Fori(1, XT_TILES // 2) as i:
                for b in range(2):
                    expert_load(i * 2 + b, b, False)
            expert_load(XT_TILES - 1, 0, False)

            for t in range(NT):
                n = P if t < NT - 1 else TAIL
                sp.wait_ge(out_ready, t + 1)
                sp.dma_start(out[t * P:t * P + n, :], x2[0:n, t, :]).then_inc(out_stored, 16)
            sp.wait_ge(out_stored, 16 * NT)

        @block.gpsimd
        def _(pool):
            g = nc.gpsimd
            g.memset(x2[:, NT - 1, :], 0.0).then_inc(x_memset, 1)
            g.memset(src_i[:, EJ:EC], 0).then_inc(edge_memset, 1)
            g.memset(dst_i[:, EJ:EC], 16 * P - 1).then_inc(edge_memset, 1)
            g.memset(typ_i[:, EJ:EC], 0).then_inc(edge_memset, 1)
            g.iota(diff[:], [[1, P]], base=0, channel_multiplier=-1,
                   allow_small_or_imprecise_dtypes=True).then_inc(pool_step, 1)
            g.memset(ones[:], 1.0).then_inc(consts, 1)
            pool.wait_ge(pool_step, 1)
            g.tensor_scalar(ident[:], diff[:], 0.0, None, ALU.is_equal).then_inc(consts, 1)
            g.tensor_scalar(below[:], diff[:], 0.0, None, ALU.is_gt).then_inc(consts, 1)
            g.iota(iota_h[:], [[1, TILES]], base=0, channel_multiplier=0,
                   allow_small_or_imprecise_dtypes=True).then_inc(consts, 1)
            g.iota(iota_f[:], [[1, P + 1]], base=0, channel_multiplier=0,
                   allow_small_or_imprecise_dtypes=True).then_inc(consts, 1)
            g.iota(tilecol[:], [[P, 4]], base=0, channel_multiplier=1,
                   allow_small_or_imprecise_dtypes=True).then_inc(consts, 1)
            g.memset(zeros_h[:], 0.0).then_inc(consts, 1)
            g.memset(slot_f[:], NO_TILE).then_inc(consts, 1)
            g.memset(mbd[:], 0.0).then_inc(consts, 1)
            g.iota(order[:], [[0, NT], [-1, NX]], base=NX, channel_multiplier=0,
                   allow_small_or_imprecise_dtypes=True).then_inc(consts, 1)
            g.iota(valid[:], [[P, NT], [0, NX]], base=0, channel_multiplier=1,
                   allow_small_or_imprecise_dtypes=True).then_inc(pool_step, 1)
            pool.wait_ge(pool_step, 2)
            g.tensor_scalar(valid[:], valid[:], float(N), None, ALU.is_lt).then_inc(consts, 1)
            pool.wait_ge(consts, 11)
            pool.dma_start(x_slots.rearrange("(t p) d -> p t d", p=P),
                           zrow.unsqueeze(1).to_broadcast([P, XT_TILES, D])).then_inc(x_zeroed, 16)

            pool.wait_ge(gidx_ready, 1)
            for n in range(4):
                pool.wait_ge(h_stored[n], 16 * (R * NT // 4))

            def gather(i):
                for h in range(2):
                    first = isinstance(i, int) and i == 0
                    if not first:
                        for k in range(HALF):
                            pool.wait_ge(gathered[k], 16 * (i * 2 + h - 1))
                    g.tensor_copy(idx_ring[:, h, :], gidx[:, bass.ds(i * GRP + h * HALF, HALF)]).then_inc(idx_copied, 1)
                    pool.wait_ge(idx_copied, i * 2 + h + 1)
                    pool.sem_inc(gather_turn, 1)
                    for k in range(HALF):
                        if not (first and h == 0):
                            pool.wait_ge(agg_done, i * GRP + (h - 1) * HALF + k + 1)
                            pool.sem_inc(gather_turn, 1)
                        g.indirect_dma_start(msg[:, k, :], None, h_table,
                                             bass.IndirectOffsetOnAxis(ap=idx_ring[:, h, k:k + 1], axis=0)
                                             ).then_inc(gathered[k], 16)

            gather(0)
            with pool.Fori(1, TILES // GRP) as i:
                gather(i)

            pool.wait_ge(slots_ready, 1)
            pool.wait_ge(xn_ready, 2 * NT)
            for t in range(NT):
                n = P if t < NT - 1 else TAIL
                for c in range(TOPK):
                    g.indirect_dma_start(x_slots, bass.IndirectOffsetOnAxis(ap=slots_i[0:n, c, t:t + 1], axis=0),
                                         xn[0:n, t, :], None).then_inc(x_scattered, 16)
            tiles_of = [(XT_TILES + 1) // 2, XT_TILES // 2]
            for b in range(2):
                pool.wait_ge(y_stored[b], 16 * tiles_of[b])
            for t in range(NT):
                n = P if t < NT - 1 else TAIL
                for c in range(TOPK):
                    q = (t * TOPK + c) % 4
                    if t >= 2:
                        pool.wait_ge(out_ready, t - 1)
                    g.indirect_dma_start(y_ring[0:n, q, :], None, y_slots,
                                         bass.IndirectOffsetOnAxis(ap=slots_i[0:n, c, t:t + 1], axis=0)
                                         ).then_inc(y_back[q], 16)

        @block.scalar
        def _(act):
            s = nc.scalar
            act.wait_ge(var_ready, 1)
            s.activation(std[:], vare[:], ACT.Sqrt).then_inc(std_ready, 1)

            def copy_transposed(t, base):
                act.wait_ge(tr_done, base + t + 1)
                s.copy(xnT[:, :, t * P:(t + 1) * P],
                       bank[t % 2][:].rearrange("p (k m) -> p k m", k=KD)).then_inc(tr_copied, 1)

            for t in range(NT):
                copy_transposed(t, 0)

            def copy_h(i):
                for h in range(2):
                    for t in range(NT):
                        n = h * NT + t
                        act.wait_ge(h_done, i * 2 * NT + n + 1)
                        if isinstance(i, int):
                            at_least(act, h_stored[n % 4], 16 * (i * 2 * NT // 4 + n // 4))
                        else:
                            act.wait_ge(h_stored[n % 4], 16 * (i * (2 * NT // 4) + n // 4))
                        s.copy(stage[:, n % 4, :], bank[2 + n % 2][:]).then_inc(h_copied, 1)

            copy_h(0)
            n = 0
            for k in range(KD):
                n += 1
                act.wait_ge(mix_done, n)
                s.copy(gram[:, k, :], bank[n % 2][:]).then_inc(mix_copied, 1)
            for k in range(KD):
                n += 1
                act.wait_ge(mix_done, n)
                s.copy(u_sb[:, k, :], bank[n % 2][:]).then_inc(mix_copied, 1)
            act.wait_ge(x_zeroed, 16)
            act.wait_ge(consts, 11)
            for k in range(KD):
                n += 1
                act.wait_ge(mix_done, n)
                for q in range(2):
                    c = s.mul(mbd[q * HEAD:(q + 1) * HEAD, k, q * HEAD:(q + 1) * HEAD],
                              bank[n % 2][q * HEAD:(q + 1) * HEAD, q * HEAD:(q + 1) * HEAD], MIX_SCALE)
                c.then_inc(mix_copied, 1)
            for k in range(KD):
                n += 1
                act.wait_ge(mix_done, n)
                s.copy(tt_sb[:, k, :], bank[n % 2][:]).then_inc(mix_copied, 1)
            with act.Fori(1, R // 2) as i:
                copy_h(i)

            def dst_one_hots(i):
                for n in range(GRP):
                    t = i * GRP + n
                    if not (isinstance(i, int) and i == 0):
                        act.wait_ge(agg_done, t - GRP + 1)
                    s.activation(dist[:, n % 2, :], iota_f[:, 1:P + 1], ACT.Square,
                                 bias=ndst[:, bass.ds(t, 1)]).then_inc(dist_ready, 1)
                    act.wait_ge(dist_ready, t + 1)
                    s.activation(oh_dst[:, n, :], dist[:, n % 2, :], ACT.Relu, scale=-1.0,
                                 bias=ones[:, 0:1]).then_inc(ohd_ready, 1)

            act.wait_ge(ndst_ready, 1)
            dst_one_hots(0)
            with act.Fori(1, TILES // GRP) as i:
                dst_one_hots(i)

            act.wait_ge(var_ready, 2)
            s.activation(std[:], vare[:], ACT.Sqrt).then_inc(std_ready, 1)
            for t in range(NT):
                copy_transposed(t, NT)
            act.wait_ge(gap_ready, 1)
            s.activation(wexp[:, 1, :], wexp[:, 0, :], ACT.Exp).then_inc(exp_ready, 1)

            def expert(sl, b):
                e = act.value_load(et_i[0:1, bass.ds(sl, 1)], min_val=0, max_val=NX - 1)
                for f in range(KF):
                    if f % 4 == 0:
                        act.wait_ge(l1_done, sl * KF + f + 4)
                    if f == 0 and not (isinstance(sl, int) and sl == 0):
                        act.wait_ge(l2_done, sl)
                    s.activation(hT[:, f, :], bank[2 + f // 4][:, (f % 4) * P:(f % 4 + 1) * P], ACT.Relu,
                                 bias=b1_sb[:, bass.ds(e * KF + f, 1)]).then_inc(l1_copied, 1)
                act.wait_ge(y_copied, sl + 1)
                act.dma_start(y_slots[bass.ds(sl * P, P), :], y_sb[:, b, :]).then_inc(y_stored[b], 16)

            act.wait_ge(et_int, 1)
            act.wait_ge(small_in, 16 * 6)
            expert(0, 0)
            expert(1, 1)
            with act.Fori(1, XT_TILES // 2) as i:
                for b in range(2):
                    expert(i * 2 + b, b)
            expert(XT_TILES - 1, 0)

        @block.tensor
        def _(pe):
            mm = nc.tensor.matmul

            def transpose_rows(t, base):
                pe.wait_ge(xn_ready, base + t + 1)
                at_least(pe, tr_copied, base + t - 1)
                for k in range(KD):
                    last = nc.tensor.transpose(bank[t % 2][:, k * P:(k + 1) * P], xn[:, t, k * P:(k + 1) * P], ident[:])
                last.then_inc(tr_done, 1)

            pe.wait_ge(consts, 11)
            for t in range(NT):
                transpose_rows(t, 0)
            pe.wait_ge(tr_copied, NT)

            def h_tile(i, h, t, between=None):
                n = h * NT + t
                if t == 0:
                    pe.wait_ge(wrel_in[h], 16 * (i + 1))
                if not (isinstance(i, int) and i * 2 * NT + n < 2):
                    pe.wait_ge(h_copied, i * 2 * NT + n - 1)
                for k in range(KD):
                    last = mm(bank[2 + n % 2][:], xnT[:, k, t * P:(t + 1) * P], wrel[:, h, k, :],
                              start=(k == 0), stop=(k == KD - 1))
                last.then_inc(h_done, 1)

            for t in range(NT):
                h_tile(0, 0, t)
            pe.wait_ge(tot_ready, NB)
            mm(bank[4][:, 0:NB], below[:], tot[:], start=True, stop=True)
            mm(bank[4][:, NB:2 * NB], ones[:], tot[:], start=True, stop=True).then_inc(off_done, 1)
            for t in range(NT):
                h_tile(0, 1, t)

            pe.wait_ge(mix_in, 16 * 5)
            n = 0

            def small(m, k_range, lhs, rhs, done, width=D):
                for j, k in enumerate(k_range):
                    last = mm(bank[m % 2][:, 0:width], lhs(k), rhs(k), start=(j == 0), stop=(j == len(k_range) - 1))
                last.then_inc(done, 1)

            for k in range(KD):
                n += 1
                at_least(pe, mix_copied, n - 2)
                small(n, range(NT), lambda t: xn[:, t, k * P:(k + 1) * P], lambda t: xn[:, t, :], mix_done)
            pe.wait_ge(mix_copied, n)
            for k in range(KD):
                n += 1
                at_least(pe, mix_copied, n - 2)
                small(n, range(KD), lambda j: gram[:, j, k * P:(k + 1) * P], lambda j: wv_sb[:, j, :], mix_done)
            pe.wait_ge(mix_copied, n)
            for k in range(KD):
                n += 1
                at_least(pe, mix_copied, n - 2)
                small(n, range(KD), lambda j: wk_sb[:, j, k * P:(k + 1) * P],
                      lambda j: u_sb[:, j, k * P:(k + 1) * P], mix_done, P)
            pe.wait_ge(mix_copied, n)
            for k in range(KD):
                n += 1
                at_least(pe, mix_copied, n - 2)
                small(n, [k], lambda j: mbd[:, j, :], lambda j: wqT_sb[:, j, :], mix_done)
            pe.wait_ge(mix_copied, n)
            for k in range(KD):
                n += 1
                if k >= 2:
                    pe.wait_ge(wtot_ready, k - 1)
                small(n, range(KD), lambda j: tt_sb[:, j, k * P:(k + 1) * P], lambda j: wout_sb[:, j, :], mix_done)
            pe.wait_ge(wtot_ready, KD)
            for t in range(NT):
                at_least(pe, base_added, t - 1)
                for k in range(KD):
                    last = mm(bank[t % 2][:], xnT[:, k, t * P:(t + 1) * P], wtot[:, k, :],
                              start=(k == 0), stop=(k == KD - 1))
                last.then_inc(base_done, 1)

            pe.wait_ge(bt_ready, 1)
            for m in range(4):
                last = mm(bank[4][0:1, m * P:(m + 1) * P], bt_col[:, m:m + 1], ident[:], start=True, stop=True)
            last.then_inc(bt_done, 1)

            def sort_column(j, k, start=False, stop=False):
                pe.wait_ge(oh_ready, j + 1)
                mm(bank[5][:, 0:TILES], oh_row[:, k, :], oh_src[:, k, :], start=start, stop=stop, skip_group_check=True)
                mm(bank[6][:, 0:TILES], oh_row[:, k, :], oh_code[:, k, :], start=start, stop=stop, skip_group_check=True)
                mm(bank[7][:, 0:NB], oh_loc[:, k, :], oh_bkt[:, k, :], start=start, stop=stop,
                   skip_group_check=True).then_inc(oh_used, 1)

            per_tile = SORT
            per_body = per_tile * 2 * NT

            def types_and_sort(i, first):
                for h in range(2):
                    for t in range(NT):
                        h_tile(i, h, t)
                        for c in range(per_tile):
                            j = (h * NT + t) * per_tile + c
                            sort_column((i - 1) * per_body + j, j % SORT, start=(first and j == 0))

            types_and_sort(1, True)
            with pe.Fori(2, R // 2) as i:
                types_and_sort(i, False)
            for j in range((R // 2 - 1) * per_body, EC):
                sort_column(j, j % SORT, stop=(j == EC - 1))

            def aggregate(i):
                for h in range(2):
                    for k in range(HALF):
                        first = isinstance(i, int) and i == 0 and h == 0
                        t = i * GRP + h * HALF + k
                        pe.wait_ge(gathered[k], 16 * (i * 2 + h + 1))
                        pe.wait_ge(ohd_ready, t + 1)
                        if not first:
                            pe.wait_ge(agg_added, 2 * (t - HALF + 1))
                        mm(bank[k][:], oh_dst[:, h * HALF + k, :], msg[:, k, :], start=True, stop=True).then_inc(agg_done, 1)

            pe.wait_ge(gidx_ready, 1)
            aggregate(0)
            with pe.Fori(1, TILES // GRP) as i:
                aggregate(i)

            pe.wait_ge(small_in, 16 * 6)
            for t in range(NT):
                transpose_rows(t, NT)
            pe.wait_ge(tr_copied, 2 * NT)
            for t in range(NT):
                for k in range(KD):
                    last = mm(bank[2][:, t * NX:(t + 1) * NX], xnT[:, k, t * P:(t + 1) * P], gate_sb[:, k, :],
                              start=(k == 0), stop=(k == KD - 1))
            last.then_inc(logit_done, 1)
            pe.wait_ge(took_ready, 1)
            mm(bank[3][:, 0:NX * NT], below[:], took[:].rearrange("p e t -> p (e t)"), start=True, stop=True)
            mm(bank[3][:, NX * NT:2 * NX * NT], ones[:], took[:].rearrange("p e t -> p (e t)"),
               start=True, stop=True).then_inc(cum_done, 1)
            pe.wait_ge(et_ready, 1)
            mm(bank[4][0:1, 0:P], et_col[:], ident[:], start=True, stop=True).then_inc(et_done, 1)
            for t in range(NT):
                pe.wait_ge(wfull_ready, 1)
                at_least(pe, wT_copied, t - 1)
                nc.tensor.transpose(bank[5][0:NX, (t % 2) * P:(t % 2 + 1) * P], wfull[:, t, :], ident[:]).then_inc(wT_done, 1)
                pe.wait_ge(wT_copied, t + 1)
                at_least(pe, b2_added, t - 1)
                mm(bank[6 + t % 2][:], wT[:, t % 2, :], b2_sb[:], start=True, stop=True).then_inc(b2_done, 1)

            def rows_of(sl, b, cnt):
                pe.wait_ge(xs_in[b], 16 * cnt)
                if not (isinstance(sl, int) and sl < 2):
                    pe.wait_ge(xT_copied, sl - 1)
                for k in range(KD):
                    last = nc.tensor.transpose(bank[b][:, k * P:(k + 1) * P], xs[:, b, k * P:(k + 1) * P], ident[:])
                last.then_inc(xT_done, 1)

            def expert(sl, b, cnt, next_cnt, ahead):
                pe.wait_ge(xT_copied, sl + 1)
                pe.wait_ge(w1_in[b], 16 * cnt)
                for f in range(KF):
                    if f % 4 == 0 and not (isinstance(sl, int) and sl == 0):
                        pe.wait_ge(l1_copied, (sl - 1) * KF + f + 4)
                    for k in range(KD):
                        last = mm(bank[2 + f // 4][:, (f % 4) * P:(f % 4 + 1) * P], ew1[b][:, k, f * P:(f + 1) * P],
                                  xsT[:, b, k, :], start=(k == 0), stop=(k == KD - 1))
                    last.then_inc(l1_done, 1)
                if ahead:
                    rows_of(sl + 1, 1 - b, next_cnt)
                pe.wait_ge(w2_in[b], 16 * cnt)
                if not (isinstance(sl, int) and sl < 2):
                    pe.wait_ge(y_copied, sl - 1)
                for f in range(KF):
                    pe.wait_ge(l1_copied, sl * KF + f + 1)
                    last = mm(bank[4 + b][:], hT[:, f, :], ew2[b][:, f, :], start=(f == 0), stop=(f == KF - 1))
                last.then_inc(l2_done, 1)

            pe.wait_ge(b2_added, NT)
            rows_of(0, 0, 1)
            expert(0, 0, 1, 1, True)
            expert(1, 1, 1, 2, True)
            with pe.Fori(1, (XT_TILES - 1) // 2) as i:
                expert(i * 2, 0, i + 1, i + 1, True)
                expert(i * 2 + 1, 1, i + 1, i + 2, True)
            for sl in range((XT_TILES - 1) // 2 * 2, XT_TILES):
                expert(sl, sl % 2, sl // 2 + 1, (sl + 1) // 2 + 1, sl + 1 < XT_TILES)

        @block.vector
        def _(dve):
            v = nc.vector
            steps = [0]

            def link(ins):
                steps[0] += 1
                ins.then_inc(dve_step, 1)
                dve.wait_ge(dve_step, steps[0])

            def layer_norm(rnd):
                for t in range(NT):
                    if rnd == 0 and t == 0:
                        dve.wait_ge(x_in, 16)
                    if rnd == 0 and t == NT - 1:
                        dve.wait_ge(x_tail_in, 16)
                        dve.wait_ge(x_memset, 1)
                    last = v.bn_stats(stats[:, t, :], x2[:, t, :])
                link(last)
                for t in range(NT):
                    last = v.bn_aggr(mv[:, t, :], stats[:, t, :])
                link(last)
                v.tensor_scalar(vare[:], mv[:, :, 1], EPS, None, ALU.add).then_inc(var_ready, 1)
                dve.wait_ge(std_ready, rnd + 1)
                link(v.reciprocal(rstd[:], std[:]))
                for t in range(NT):
                    v.tensor_scalar(xn[:, t, :], x2[:, t, :], mv[:, t, 0:1], rstd[:, t:t + 1],
                                    ALU.subtract, ALU.mult).then_inc(xn_ready, 1)

            layer_norm(0)
            dve.wait_ge(small_in, 16 * 6)
            link(v.tensor_tensor(bias_row[:, 0, :], bias_row[:, 0, :], bias_row[:, 1, :], ALU.add))
            dve.wait_ge(xn_ready, NT)
            for t in range(NT):
                last = v.tensor_tensor(x2[:, t, :], x2[:, t, :], bias_row[:, 0, :], ALU.add)
            link(last)

            dve.wait_ge(edges_in, 16 * 6)
            dve.wait_ge(edge_memset, 3)
            link(v.tensor_scalar(tmp_i[:], dst_i[:], P - 1, None, ALU.bitwise_and))
            v.tensor_copy(src_f[:], src_i[:])
            link(v.tensor_copy(dloc_f[:], tmp_i[:]))
            link(v.scalar_tensor_tensor(code_f[:], typ_i[:], float(P), dloc_f[:], ALU.mult, ALU.add))
            link(v.tensor_scalar(code_f[:], code_f[:], 1024.0, None, ALU.add))
            link(v.tensor_scalar(tmp_i[:], dst_i[:], 7, None, ALU.arith_shift_right))
            link(v.scalar_tensor_tensor(bkt_f[:], tmp_i[:], float(R), typ_i[:], ALU.mult, ALU.add))
            link(v.tensor_copy(bkt_h[:], bkt_f[:]))

            dve.wait_ge(consts, 11)
            def count_buckets(i):
                for q in range(2):
                    b = i * 2 + q
                    at_least(dve, tot_ready, b - 1)
                    v.tensor_scalar(eq_h[:, q, :], bkt_h[:], iota_f[:, bass.ds(b, 1)], None, ALU.is_equal,
                                    ALU.add, accum_out=tot[:, bass.ds(b, 1)]).then_inc(tot_ready, 1)

            count_buckets(0)
            with dve.Fori(1, NB // 2) as i:
                count_buckets(i)

            dve.wait_ge(off_done, 1)
            n_tiles, end_tile, start_tile, from_0 = (cols[:, n, :] for n in range(4))
            link(v.tensor_scalar(cols_i[:, 0, :], bank[4][:, NB:2 * NB], float(P - 1), None, ALU.add))
            link(v.tensor_scalar(cols_i[:, 1, :], cols_i[:, 0, :], 7, None, ALU.arith_shift_right))
            link(v.tensor_copy(n_tiles, cols_i[:, 1, :]))
            link(v.tensor_tensor_scan(end_tile, n_tiles, zeros_h[:, 0:NB], 0.0, ALU.add, ALU.add))
            link(v.tensor_tensor(start_tile, end_tile, n_tiles, ALU.subtract))
            link(v.scalar_tensor_tensor(from_0, start_tile, float(P), bank[4][:, 0:NB], ALU.mult, ALU.add))
            link(v.tensor_scalar(rank_from[:], from_0, -1.0, None, ALU.add))
            for m in range(4):
                last = v.tensor_scalar(bt_junk[:, m, :], end_tile, tilecol[:, m:m + 1], None, ALU.is_le, ALU.add,
                                       accum_out=bt_col[:, m:m + 1])
            last.then_inc(bt_ready, 1)

            def rank_buckets(i):
                for q in range(2):
                    b = i * 2 + q
                    at_least(dve, slots_set, b - 1)
                    v.tensor_scalar(eq_h[:, q, :], bkt_h[:], iota_f[:, bass.ds(b, 1)], None, ALU.is_equal).then_inc(rank1, 1)
                for q in range(2):
                    b = i * 2 + q
                    dve.wait_ge(rank1, b + 1)
                    v.tensor_tensor_scan(rank_f[:, q, :], eq_h[:, q, :], zeros_h[:], rank_from[:, bass.ds(b, 1)],
                                         ALU.add, ALU.add).then_inc(rank2, 1)
                for q in range(2):
                    b = i * 2 + q
                    at_least(dve, slots_set, b)
                    dve.wait_ge(rank2, b + 1)
                    dve.sem_inc(copy_turn, 1)
                    v.copy_predicated(slot_f[:], eq_h[:, q, :].bitcast(mybir.dt.int16), rank_f[:, q, :]).then_inc(slots_set, 1)

            dve.wait_ge(tot_ready, NB)
            rank_buckets(0)
            with dve.Fori(1, NB // 2) as i:
                rank_buckets(i)
            dve.wait_ge(slots_set, NB)
            link(v.tensor_copy(slot_i[:], slot_f[:]))
            link(v.tensor_scalar(tmp_i[:], slot_i[:], P - 1, None, ALU.bitwise_and))
            link(v.tensor_copy(row_f, tmp_i[:]))
            link(v.tensor_scalar(tmp_i[:], slot_i[:], 7, None, ALU.arith_shift_right))
            link(v.tensor_copy(tile_f, tmp_i[:]))

            for k in range(KD):
                dve.wait_ge(mix_done, 4 * KD + k + 1)
                v.tensor_tensor(wtot[:, k, :], bank[(4 * KD + k + 1) % 2][:], wself_sb[:, k, :], ALU.add).then_inc(wtot_ready, 1)
            for t in range(NT):
                dve.wait_ge(base_done, t + 1)
                v.tensor_tensor(x2[:, t, :], x2[:, t, :], bank[t % 2][:], ALU.add).then_inc(base_added, 1)

            dve.wait_ge(bt_done, 1)
            link(v.tensor_scalar(bt_i[:, 0, :], bank[4][0:1, :], float(NB - 1), None, ALU.min))
            link(v.tensor_scalar(bt_i[:, 1, :], bt_i[:, 0, :], 3, None, ALU.arith_shift_right))

            def one_hots(j, k):
                if not (isinstance(j, int) and j < SORT):
                    dve.wait_ge(oh_used, j - SORT + 1)
                v.tensor_scalar(oh_row[:, k, :], iota_h[:, 0:P], row_f[:, bass.ds(j, 1)], None, ALU.is_equal)
                v.tensor_scalar(oh_loc[:, k, :], iota_h[:, 0:P], dloc_f[:, bass.ds(j, 1)], None, ALU.is_equal)
                v.tensor_scalar(oh_bkt[:, k, :], iota_h[:, 0:NB], bkt_f[:, bass.ds(j, 1)], None, ALU.is_equal)
                v.tensor_scalar(oh_src[:, k, :], iota_h[:], tile_f[:, bass.ds(j, 1)], src_f[:, bass.ds(j, 1)],
                                ALU.is_equal, ALU.mult)
                v.tensor_scalar(oh_code[:, k, :], iota_h[:], tile_f[:, bass.ds(j, 1)], code_f[:, bass.ds(j, 1)],
                                ALU.is_equal, ALU.mult).then_inc(oh_ready, 1)

            for k in range(SORT):
                one_hots(k, k)
            with dve.Fori(1, EC // SORT) as i:
                for k in range(SORT):
                    one_hots(i * SORT + k, k)
            for j in range(EC // SORT * SORT, EC):
                one_hots(j, j % SORT)

            dve.wait_ge(oh_used, EC)
            link(v.tensor_scalar(inv_cnt[:], bank[7][:, 0:NB], 1.0, None, ALU.max))
            link(v.reciprocal(inv_cnt[:], inv_cnt[:]))
            link(v.tensor_copy(code_i, bank[6][:, 0:TILES]))
            link(v.tensor_scalar(part_i[:, 0, :], code_i, 7, R - 1, ALU.arith_shift_right, ALU.bitwise_and))
            v.scalar_tensor_tensor(gidx[:], part_i[:, 0, :], float(NPAD), bank[5][:, 0:TILES], ALU.mult, ALU.add).then_inc(gidx_ready, 1)
            dve.wait_ge(gidx_ready, 1)
            v.tensor_scalar(part_i[:, 0, :], code_i, P - 1, None, ALU.bitwise_and)
            link(v.tensor_scalar(part_i[:, 1, :], code_i, 10, None, ALU.arith_shift_right))
            v.scalar_tensor_tensor(ndst[:], part_i[:, 1, :], -1.0, part_i[:, 0, :], ALU.mult, ALU.subtract).then_inc(ndst_ready, 1)

            def add_messages(i):
                _, buckets = nc.values_load_multi_w_load_instructions(
                    bt_i[0:1, 0, bass.ds(i * GRP, GRP)], engines=[mybir.EngineType.DVE], min_val=0, max_val=NB - 1)
                for n in range(GRP):
                    t = i * GRP + n
                    bucket = buckets[n]
                    row = dve.snap(bucket // R * D)
                    for h in range(2):
                        if h == 0:
                            dve.wait_ge(agg_done, t + 1)
                        at_least(dve, agg_added, 2 * t + h - 1)
                        into = x2_flat[:, bass.ds(row + h * (D // 2), D // 2)]
                        v.scalar_tensor_tensor(into, bank[n % HALF][:, h * (D // 2):(h + 1) * (D // 2)],
                                               inv_cnt[:, bass.ds(bucket, 1)], into, ALU.mult, ALU.add).then_inc(agg_added, 1)

            x2_flat = x2[:].rearrange("p t d -> p (t d)")
            add_messages(0)
            with dve.Fori(1, TILES // GRP) as i:
                add_messages(i)
            dve.wait_ge(agg_added, 2 * TILES)

            layer_norm(1)

            dve.wait_ge(logit_done, 1)
            link(v.tensor_tensor(logit[:], bank[2][:, 0:NT * NX].rearrange("p (t e) -> p t e", t=NT),
                                 gb_row[:].unsqueeze(1).to_broadcast([P, NT, NX]), ALU.add))
            values = logit
            for c in range(TOPK):
                link(v.tensor_reduce(top[:, c, :], values[:], AX_X, ALU.max))
                link(v.tensor_tensor(score[:], values[:], top[:, c, :].unsqueeze(2).to_broadcast([P, NT, NX]), ALU.is_equal))
                link(v.tensor_tensor(score[:], score[:], order[:], ALU.mult))
                link(v.tensor_reduce(best[:], score[:], AX_X, ALU.max))
                link(v.tensor_tensor(pick[:, c], order[:], best[:].unsqueeze(2).to_broadcast([P, NT, NX]), ALU.is_equal))
                if c == 0:
                    link(v.tensor_scalar(masked[:], pick[:, 0], -3e38, 1.5e38, ALU.mult, ALU.add))
                    link(v.tensor_tensor(masked[:], masked[:], logit[:], ALU.min))
                    values = masked
            v.tensor_tensor(wexp[:, 0, :], top[:, 1, :], top[:, 0, :], ALU.subtract).then_inc(gap_ready, 1)
            for c in range(TOPK):
                link(v.tensor_tensor(pick[:, c], pick[:, c], valid[:], ALU.mult))
            v.tensor_tensor(took[:].rearrange("p e t -> p t e"), pick[:, 0], pick[:, 1], ALU.add).then_inc(took_ready, 1)
            dve.wait_ge(exp_ready, 1)
            link(v.tensor_scalar(wexp[:, 2, :], wexp[:, 1, :], 1.0, None, ALU.add))
            link(v.reciprocal(wts[:, 0, :], wexp[:, 2, :]))
            link(v.tensor_tensor(wts[:, 1, :], wexp[:, 1, :], wts[:, 0, :], ALU.mult))
            v.tensor_tensor(wfull[:], pick[:, 0], wts[:, 0, :].unsqueeze(2).to_broadcast([P, NT, NX]), ALU.mult)
            link(v.tensor_tensor(wpart[:], pick[:, 1], wts[:, 1, :].unsqueeze(2).to_broadcast([P, NT, NX]), ALU.mult))
            v.tensor_tensor(wfull[:], wfull[:], wpart[:], ALU.add).then_inc(wfull_ready, 1)

            dve.wait_ge(cum_done, 1)
            within = bank[3][:, 0:NX * NT].rearrange("p (e t) -> p e t", e=NX)
            per_tile = bank[3][:, NX * NT:2 * NX * NT].rearrange("p (e t) -> p e t", e=NX)
            x_count, x_tiles, x_end, x_from = (xcols[:, n, :] for n in range(4))
            link(v.tensor_copy(tsum[:], per_tile))
            link(v.tensor_reduce(x_count, tsum[:], AX_X, ALU.add))
            link(v.tensor_tensor_scan(tcum[:].rearrange("p e t -> p (e t)"), tsum[:].rearrange("p e t -> p (e t)"),
                                      zeros_h[:, 0:NX * NT], 0.0, ALU.add, ALU.add))
            link(v.tensor_tensor(tcum[:], tcum[:], tsum[:], ALU.subtract))
            link(v.tensor_scalar(xcols_i[:], x_count, float(P - 1), None, ALU.add))
            link(v.tensor_scalar(xcols_i[:], xcols_i[:], 7, None, ALU.arith_shift_right))
            link(v.tensor_copy(x_tiles, xcols_i[:]))
            link(v.tensor_tensor_scan(x_end, x_tiles, zeros_h[:, 0:NX], 0.0, ALU.add, ALU.add))
            link(v.tensor_scalar(et_junk[:], x_end, tilecol[:, 0:1], None, ALU.is_le, ALU.add, accum_out=et_col[:]))
            v.tensor_scalar(et_col[:], et_col[:], float(NX - 1), None, ALU.min).then_inc(et_ready, 1)
            link(v.tensor_tensor(x_from, x_end, x_tiles, ALU.subtract))
            link(v.scalar_tensor_tensor(x_from, x_from, float(P), tcum[:, :, 0], ALU.mult, ALU.subtract))
            link(v.tensor_tensor(xslot[:], tcum[:], within, ALU.add))
            link(v.tensor_tensor(xslot[:], xslot[:], x_from.unsqueeze(2).to_broadcast([P, NX, NT]), ALU.add))
            for c in range(TOPK):
                link(v.tensor_tensor(pick_slot[:], pick[:, c], xslot[:].rearrange("p e t -> p t e"), ALU.mult))
                link(v.tensor_reduce(slots_f[:, c, :], pick_slot[:], AX_X, ALU.add))
            v.tensor_copy(slots_i[:], slots_f[:]).then_inc(slots_ready, 1)
            dve.wait_ge(et_done, 1)
            v.tensor_copy(et_i[:], bank[4][0:1, 0:P]).then_inc(et_int, 1)

            for t in range(NT):
                dve.wait_ge(wT_done, t + 1)
                at_least(dve, b2_done, t - 1)
                v.tensor_copy(wT[:, t % 2, :], bank[5][0:NX, (t % 2) * P:(t % 2 + 1) * P]).then_inc(wT_copied, 1)
                dve.wait_ge(b2_done, t + 1)
                v.tensor_tensor(x2[:, t, :], x2[:, t, :], bank[6 + t % 2][:], ALU.add).then_inc(b2_added, 1)

            def copy_rows(sl, b):
                dve.wait_ge(xT_done, sl + 1)
                if not (isinstance(sl, int) and sl < 2):
                    dve.wait_ge(l1_done, (sl - 1) * KF)
                v.tensor_copy(xsT[:, b], bank[b][:].rearrange("p (k m) -> p k m", k=KD)).then_inc(xT_copied, 1)

            def copy_y(sl, b, cnt):
                dve.wait_ge(l2_done, sl + 1)
                at_least(dve, y_stored[b], 16 * cnt)
                v.tensor_copy(y_sb[:, b, :], bank[4 + b][:]).then_inc(y_copied, 1)

            copy_rows(0, 0)
            copy_rows(1, 1)
            copy_y(0, 0, 0)
            copy_rows(2, 0)
            copy_y(1, 1, 0)
            with dve.Fori(1, (XT_TILES - 1) // 2) as i:
                copy_rows(i * 2 + 1, 1)
                copy_y(i * 2, 0, i)
                copy_rows(i * 2 + 2, 0)
                copy_y(i * 2 + 1, 1, i)
            copy_y(XT_TILES - 1, 0, XT_TILES // 2)

            for t in range(NT):
                for c in range(TOPK):
                    q = (t * TOPK + c) % 4
                    n = P if t < NT - 1 else TAIL
                    dve.wait_ge(y_back[q], 16 * ((t * TOPK + c) // 4 + 1))
                    ins = v.scalar_tensor_tensor(x2[0:n, t, :], y_ring[0:n, q, :], wts[0:n, c, t:t + 1], x2[0:n, t, :],
                                                 ALU.mult, ALU.add)
                    if c == 0:
                        link(ins)
                ins.then_inc(out_ready, 1)


_INS = ["x", "src", "dst", "edge_type", "w_self_t", "w_rel_t", "gnn_bias", "w_q_t", "w_k", "w_v", "w_out", "b_out",
        "gate_w", "gate_b", "w1", "b1_cols", "w2", "b2"]


def kernel(x, src, dst, edge_type_8, L0_gnn_W_self, L0_gnn_W_rel, L0_gnn_bias, L0_mix_w_qkv, L0_mix_w_out,
           L0_mix_b_out, L0_ffn_gate_w, L0_ffn_gate_b, L0_ffn_w1, L0_ffn_b1, L0_ffn_w2, L0_ffn_b2):
    import numpy as np
    import concourse.bacc as bacc
    from concourse.bass_utils import run_bass_kernel_spmd

    x = np.asarray(x)
    dim = x.shape[1]
    qkv = np.asarray(L0_mix_w_qkv)
    b1 = np.asarray(L0_ffn_b1)
    laid = dict(zip(_INS, [
        x, src, dst, edge_type_8,
        np.asarray(L0_gnn_W_self).T, np.asarray(L0_gnn_W_rel).transpose(0, 2, 1), L0_gnn_bias,
        qkv[:, 0:dim].T, qkv[:, dim:2 * dim], qkv[:, 2 * dim:3 * dim], L0_mix_w_out, L0_mix_b_out,
        L0_ffn_gate_w, L0_ffn_gate_b, L0_ffn_w1,
        b1.reshape(b1.shape[0], -1, P).transpose(2, 0, 1).reshape(P, -1),
        L0_ffn_w2, L0_ffn_b2]))
    nc = bacc.Bacc("TRN2", target_bir_lowering=False, num_devices=1)
    arrays, args = {}, []
    for name in _INS:
        a = np.ascontiguousarray(laid[name])
        arrays[f"in_{name}"] = a
        args.append(nc.dram_tensor(f"in_{name}", a.shape, mybir.dt.from_np(a.dtype), kind="ExternalInput").ap())
    out = nc.dram_tensor("out_0", x.shape, F32, kind="ExternalOutput").ap()
    gnn_moe_kernel(nc, *args, out)
    return run_bass_kernel_spmd(nc, [arrays], core_ids=[0]).results[0]["out_0"]
```

```python
from contextlib import ExitStack

import concourse.bass as bass
from concourse import mybir

ALU = mybir.AluOpType
ACT = mybir.ActivationFunctionType
AX_X = mybir.AxisListType.X
F32 = mybir.dt.float32
F32R = mybir.dt.float32r
F16 = mybir.dt.float16
BF16 = mybir.dt.bfloat16
I32 = mybir.dt.int32

P = 128


def gnn_moe_kernel(nc, x, src, dst, etype, w_self_t, w_rel_t, gnn_bias, w_q_t, w_k, w_v, w_out, b_out,
                   gate_w, gate_b, w1, b1, w2, b2, out):
    N, D = x.shape
    KD = D // P
    NT = (N + P - 1) // P
    TAIL = N - (NT - 1) * P
    NPAD = NT * P
    R = w_rel_t.shape[0]
    E = src.shape[0]
    EJ = E // P
    ETAIL = E - EJ * P
    EC = EJ + (ETAIL > 0)
    NB = NT * R
    HALF = 7
    GRP = 2 * HALF
    TILES = -(-((E + NB * (P - 1)) // P) // GRP) * GRP
    NX = w1.shape[0]
    F = w1.shape[2]
    KF = F // P
    TOPK = 2
    XT_TILES = (TOPK * N + NX * (P - 1)) // P
    EPS = 1e-5
    HEAD = 64
    MIX_SCALE = (1.0 / float(HEAD) ** 0.5) / N
    BACK = 8
    SORT = 6
    PAIR = 2 * NT
    PAIR_COLUMNS = -(-EC // (R // 2 - 1) // SORT) * SORT
    FIRST_COLUMNS = EC // SORT * SORT - (R // 2 - 2) * PAIR_COLUMNS
    BARE = 4
    NO_TILE = float(P * 500)
    assert XT_TILES % 2 == 1 and FIRST_COLUMNS > SORT and TILES <= 512

    h_table = nc.dram_tensor("h_table", [R * NPAD, D], F32).ap()
    x_slots = nc.dram_tensor("x_slots", [XT_TILES * P, D], F32).ap()
    y_slots = nc.dram_tensor("y_slots", [XT_TILES * P, D], F32).ap()

    with ExitStack() as ctx:
        def sb(name, shape, dt=F32):
            return ctx.enter_context(nc.sbuf_tensor(name, shape, dt))

        def sem(name):
            return ctx.enter_context(nc.semaphore(name))

        x2 = sb("x2", [P, NT, D])
        weights_at = nc.sbuf_base
        arena = sb("arena", [P, 8, KD * D])
        xn = sb("xn", [P, NT, D])
        xnT_at = nc.sbuf_base
        sb("xnT_room", [P, KD, NPAD])
        xnT_lo_at = nc.sbuf_base
        sb("xnT_lo_room", [P, KD, NPAD])
        sb("weights_room", [P, 2 * 4 * KD * F - 8 * KD * D - NT * D - 2 * KD * NPAD])
        assert nc.sbuf_base - weights_at == 2 * 4 * KD * F * 4
        wk_sb, wv_sb, wqT_sb, wout_sb, wself_sb, gram, u_sb, tt_sb = (
            arena[:, n, :].rearrange("p (k d) -> p k d", k=KD) for n in range(8))
        wtot = gram
        base_ring = wself_sb

        def alias(name, shape, dt, offset):
            return nc.alloc_sbuf_tensor_at(name, shape, dt, offset=offset)

        BLOCK = KD * D * 4
        xnT_hi = alias("xnT_hi", [P, KD, NPAD], F32R, xnT_at)
        xnT_raw = alias("xnT_raw", [P, KD, NPAD], F32, xnT_lo_at)
        xnT_lo = alias("xnT_lo", [P, KD, NPAD], F32R, xnT_lo_at)
        wrel_raw = [alias(f"wrel_raw{b}", [P, KD, D], F32, weights_at + b * BLOCK) for b in range(2)]
        wrel_lo = [alias(f"wrel_lo{b}", [P, KD, D], F32R, weights_at + b * BLOCK) for b in range(2)]
        wrel_hi = [alias("wrel_hi0", [P, KD, D], F32R, weights_at + 6 * BLOCK),
                   alias("wrel_hi1", [P, KD, D], F32R, weights_at + 3 * BLOCK)]
        stage = arena[:, 2, :].rearrange("p (s d) -> p s d", s=4)
        wtot_hi = alias("wtot_hi", [P, KD, D], F32R, weights_at + 7 * BLOCK)
        wtot_lo = alias("wtot_lo", [P, KD, D], F32R, weights_at + 5 * BLOCK)
        tiles_at = nc.sbuf_base
        src_i = sb("src_i", [P, EC], I32)
        dst_i = sb("dst_i", [P, EC], I32)
        typ_i = sb("typ_i", [P, EC], I32)
        tmp_i = sb("tmp_i", [P, EC], I32)
        src_f = sb("src_f", [P, EC])
        dloc_f = sb("dloc_f", [P, EC])
        code_f = sb("code_f", [P, EC])
        bkt_f = sb("bkt_f", [P, EC])
        bkt_h = sb("bkt_h", [P, EC], BF16)
        slot_f = sb("slot_f", [P, EC])
        slot_i = src_i
        row_f = dst_i[:].bitcast(F32)
        tile_f = typ_i[:].bitcast(F32)
        widths = [P, P, P, NB, TILES]
        work = sb("work", [P, max(SORT * sum(widths) // 2, HALF * D + GRP * P)])
        half = work[:, 0:SORT * sum(widths) // 2].bitcast(F16)
        row_src, row_code, oh_loc, oh_bkt, oh_tile = (
            half[:, SORT * sum(widths[:n]):SORT * sum(widths[:n + 1])].rearrange("p (s n) -> p s n", s=SORT)
            for n in range(5))
        bias_row = work[:, 0:2 * D].rearrange("p (s d) -> p s d", s=2)
        rank_f = work[:, 2 * D:2 * D + 2 * EC].rearrange("p (s j) -> p s j", s=2)
        eq_h = work[:, 4 * D:4 * D + EC].bitcast(BF16).rearrange("p (s j) -> p s j", s=2)
        bt_junk = work[:, 5 * D:5 * D + 4 * NB].rearrange("p (m b) -> p m b", m=4)
        zrow = work[:, 6 * D:7 * D]
        mbd = work[:, 7 * D:8 * D].rearrange("p (k m) -> p k m", k=KD)
        logit_t = work[0:NX, 0:NPAD]
        msg = work[:, 0:HALF * D].rearrange("p (s d) -> p s d", s=HALF)
        oh_dst = work[:, HALF * D:HALF * D + GRP * P].rearrange("p (s n) -> p s n", s=GRP)
        tiles_end = nc.sbuf_base
        zeros_h = sb("zeros_h", [P, EC], BF16)
        tot = sb("tot", [P, NB])
        cols = sb("cols", [P, 6, NB])
        cols_i = sb("cols_i", [P, 2, NB], I32)
        rank_from = sb("rank_from", [P, NB])
        inv_cnt = sb("inv_cnt", [P, NB])
        tilecol = sb("tilecol", [P, 4])
        bt_col = sb("bt_col", [P, 4])
        bt_f = sb("bt_f", [1, 4 * P])
        bt_pair = sb("bt_pair", [1, 2 * P], I32)
        iota_h = sb("iota_h", [P, TILES], F16)
        iota_f = sb("iota_f", [P, P + 1])
        dist = sb("dist", [P, 2, P])
        diff = sb("diff", [P, P])
        ident = sb("ident", [P, P])
        below = sb("below", [P, P])
        ones = sb("ones", [P, P])
        code_i = arena[:, 1, 0:TILES].bitcast(I32)
        part_i = arena[:, 1, TILES:3 * TILES].bitcast(I32).rearrange("p (a t) -> p a t", a=2)
        gidx = sb("gidx", [P, TILES], I32)
        ndst = sb("ndst", [P, TILES])
        idx_ring = sb("idx_ring", [P, 2, HALF], I32)
        stats = sb("stats", [P, NT, 6])
        mv = sb("mv", [P, NT, 2])
        vare = sb("vare", [P, NT])
        std = sb("std", [P, NT])
        rstd = sb("rstd", [P, NT])
        gate_sb = sb("gate_sb", [P, KD, NX])
        gate_hi = sb("gate_hi", [P, KD, NX], F32R)
        gate_lo = sb("gate_lo", [P, KD, NX], F32R)
        gb_row = sb("gb_row", [P, NX])
        b2_row = sb("b2_row", [P, 2, D])
        logit = sb("logit", [P, NT, NX])
        masked = sb("masked", [P, NT, NX])
        pick = sb("pick", [P, 2, NT, NX])
        score = sb("score", [P, NT, NX])
        order = sb("order", [P, NT, NX])
        valid = sb("valid", [P, NT, NX])
        top = sb("top", [P, 2, NT])
        best = sb("best", [P, NT])
        wexp = sb("wexp", [P, 3, NT])
        wts = sb("wts", [P, 2, NT])
        took = sb("took", [P, NX, NT])
        tsum = sb("tsum", [P, NX, NT])
        tcum = sb("tcum", [P, NX, NT])
        xslot = sb("xslot", [P, NX, NT])
        xcols = sb("xcols", [P, 6, NX])
        xcols_i = sb("xcols_i", [P, NX], I32)
        pick_slot = sb("pick_slot", [P, NT, NX])
        slots_f = sb("slots_f", [P, 2, NT])
        slots_i = sb("slots_i", [P, 2, NT], I32)
        et_col = sb("et_col", [P, 1])
        et_junk = sb("et_junk", [P, NX])
        et_i = sb("et_i", [1, P], I32)
        x_end_i = sb("x_end_i", [1, NX], I32)

        bank = [ctx.enter_context(nc.psum_tensor(f"bank{n}", [P, 512], F32)) for n in range(8)]

        x_in = [sem("x_in0"), sem("x_in1")]
        x_tail_in = sem("x_tail_in")
        edges_in = sem("edges_in")
        wrel_rounded = sem("wrel_rounded")
        wrel_ready = sem("wrel_ready")
        xnT_raw_in = sem("xnT_raw_in")
        xnT_ready = sem("xnT_ready")
        wtot_rounded = sem("wtot_rounded")
        wtot_split = sem("wtot_split")
        loc_dist = sem("loc_dist")
        loc_ready = sem("loc_ready")
        wrel_in = [sem("wrel_in0"), sem("wrel_in1")]
        mix_in = sem("mix_in")
        small_in = sem("small_in")
        edge_memset = sem("edge_memset")
        x_memset = sem("x_memset")
        consts = sem("consts")
        pool_step = sem("pool_step")
        dve_step = sem("dve_step")
        std_ready = sem("std_ready")
        var_ready = sem("var_ready")
        xn_ready = sem("xn_ready")
        tr_done = sem("tr_done")
        tr_copied = sem("tr_copied")
        h_done = sem("h_done")
        h_copied = sem("h_copied")
        h_stored = [sem(f"h_stored{n}") for n in range(4)]
        tot_ready = sem("tot_ready")
        off_done = sem("off_done")
        mix_done = sem("mix_done")
        mix_copied = sem("mix_copied")
        low_done = sem("low_done")
        low_copied = sem("low_copied")
        wtot_ready = sem("wtot_ready")
        bias_ready = sem("bias_ready")
        x_biased = sem("x_biased")
        base_done = sem("base_done")
        base_copied = sem("base_copied")
        base_added = sem("base_added")
        rank1 = sem("rank1")
        rank2 = sem("rank2")
        slots_set = sem("slots_set")
        copy_turn = sem("copy_turn")
        oh_ready = sem("oh_ready")
        oh_used = sem("oh_used")
        bt_ready = sem("bt_ready")
        bt_done = sem("bt_done")
        gidx_ready = sem("gidx_ready")
        idx_copied = sem("idx_copied")
        gather_turn = sem("gather_turn")
        gathered = [sem(f"gathered{n}") for n in range(HALF)]
        ndst_ready = sem("ndst_ready")
        dist_ready = sem("dist_ready")
        ohd_ready = sem("ohd_ready")
        agg_done = sem("agg_done")
        agg_added = sem("agg_added")
        gate_rounded = sem("gate_rounded")
        gate_ready = sem("gate_ready")
        tr_rounded = sem("tr_rounded")
        lt_done = sem("lt_done")
        lt_copied = sem("lt_copied")
        logit_done = sem("logit_done")
        gap_ready = sem("gap_ready")
        exp_ready = sem("exp_ready")
        wts_ready = sem("wts_ready")
        took_ready = sem("took_ready")
        cum_done = sem("cum_done")
        slots_ready = sem("slots_ready")
        et_ready = sem("et_ready")
        et_done = sem("et_done")
        et_int = sem("et_int")
        x_zeroed = sem("x_zeroed")
        x_scattered = sem("x_scattered")
        w1_in = [sem("w1_in0"), sem("w1_in1")]
        w2_in = [sem("w2_in0"), sem("w2_in1")]
        b2_in = [sem("b2_in0"), sem("b2_in1")]
        b1_in = [sem("b1_in0"), sem("b1_in1")]
        w1_rounded = sem("w1_rounded")
        w2_rounded = sem("w2_rounded")
        split_turn = sem("split_turn")
        w1_ready = sem("w1_ready")
        w2_ready = sem("w2_ready")
        w1_used = sem("w1_used")
        w2_used = sem("w2_used")
        xs_in = [sem("xs_in0"), sem("xs_in1")]
        xT_done = sem("xT_done")
        x_hi = sem("x_hi")
        x_lo = sem("x_lo")
        l1_half_done = sem("l1_half_done")
        hid_ready = sem("hid_ready")
        hT_done = sem("hT_done")
        h_hi = sem("h_hi")
        h_lo = sem("h_lo")
        y_copied = sem("y_copied")
        y_stored = [sem("y_stored0"), sem("y_stored1")]
        y_back = [sem(f"y_back{n}") for n in range(BACK)]
        out_ready = sem("out_ready")
        out_stored = sem("out_stored")

        at = [tiles_at]

        def over(name, shape, dt=F32):
            size = 4
            for n in shape[1:]:
                size *= n
            at[0] += size
            return nc.alloc_sbuf_tensor_at(name, shape, dt, offset=at[0] - size)

        PART = KD * F

        def part(name, n):
            return nc.alloc_sbuf_tensor_at(name, [P, 5, PART], F32R, offset=weights_at + n * PART * 4)

        def loaded(name, b, n):
            return nc.alloc_sbuf_tensor_at(name, [P, PART], F32, offset=weights_at + (4 * b + n) * PART * 4)

        w1_hi, w2_hi, w1_lo, w2_lo = (part(f"weights{n}", n) for n in range(4))
        w1_raw = [loaded(f"w1_raw{b}", b, 2) for b in range(2)]
        w2_raw = [loaded(f"w2_raw{b}", b, 3) for b in range(2)]
        b1_row = over("b1_row", [P, 2, F])
        xs = over("xs", [P, 2, D])
        xT_hi = over("xT_hi", [P, KD, P], F32R)
        xT_lo = over("xT_lo", [P, KD, P], F32R)
        hid = over("hid", [P, F])
        hT_hi = over("hT_hi", [P, KF, P], F32R)
        hT_lo = over("hT_lo", [P, KF, P], F32R)
        y_sb = over("y_sb", [P, 2, D])
        assert at[0] <= tiles_end
        y_ring = arena[:].rearrange("p a n -> p (a n)")[:, 0:BACK * D].rearrange("p (s d) -> p s d", s=BACK)

        def columns_after(i, n):
            if isinstance(i, int) and i == 1:
                bare, count, start = BARE, FIRST_COLUMNS, 0
            else:
                bare, count, start = 0, PAIR_COLUMNS, FIRST_COLUMNS + (i - 2) * PAIR_COLUMNS
            if n < bare:
                return []
            columns = range((n - bare) * count // (PAIR - bare), (n + 1 - bare) * count // (PAIR - bare))
            return [(start + c, c % SORT) for c in columns]

        def low(j):
            return bank[(2, 3, 5)[j - 1]][:, 0:j * P]

        HALVES = [range(0, NT // 2), range(NT // 2, NT)]

        def square_roots(act, rnd):
            for h, tiles in enumerate(HALVES):
                part = slice(tiles[0], tiles[-1] + 1)
                act.wait_ge(var_ready, 2 * rnd + h + 1)
                nc.scalar.activation(std[:, part], vare[:, part], ACT.Sqrt).then_inc(std_ready, 1)

        LOGIT_CHUNKS = [range(t, min(t + 4, NT)) for t in range(0, NT, 4)]
        LOGITS_AFTER = [min(chunk[-1] + 2, NT - 1) for chunk in LOGIT_CHUNKS]

        LAST_COLUMNS = [(j, j % SORT) for j in range(EC // SORT * SORT, EC)]

        block = ctx.enter_context(nc.Block())

        def at_least(eng, s, value):
            if not (isinstance(value, int) and value <= 0):
                eng.wait_ge(s, value)

        @block.sync
        def _(sp):
            sp.dma_start(src_i[:, 0:EJ], src[0:EJ * P].rearrange("(p j) -> p j", p=P)).then_inc(edges_in, 16)
            sp.dma_start(dst_i[:, 0:EJ], dst[0:EJ * P].rearrange("(p j) -> p j", p=P)).then_inc(edges_in, 16)
            sp.dma_start(typ_i[:, 0:EJ], etype[0:EJ * P].rearrange("(p j) -> p j", p=P)).then_inc(edges_in, 16)
            sp.wait_ge(edge_memset, 3)
            for t_sb, t_dram in ((src_i, src), (dst_i, dst), (typ_i, etype)):
                sp.dma_start(t_sb[0:ETAIL, EJ:EC], t_dram[EJ * P:E].rearrange("(p j) -> p j", j=1)).then_inc(edges_in, 16)
            for h, (t0, t1) in enumerate(((0, NT // 2), (NT // 2, NT - 1))):
                sp.dma_start(x2[:, t0:t1, :], x[t0 * P:t1 * P, :].rearrange("(t p) d -> p t d", p=P)).then_inc(x_in[h], 16)
            sp.wait_ge(x_memset, 1)
            sp.dma_start(x2[0:TAIL, NT - 1, :], x[(NT - 1) * P:N, :]).then_inc(x_tail_in, 16)
            sp.dma_start(bias_row[:, 0, :], gnn_bias.partition_broadcast(P)).then_inc(small_in, 16)
            sp.dma_start(bias_row[:, 1, :], b_out.partition_broadcast(P)).then_inc(small_in, 16)
            sp.dma_start(gb_row[:], gate_b.partition_broadcast(P)).then_inc(small_in, 16)
            sp.dma_start(gate_sb[:], gate_w.rearrange("(k p) e -> p k e", p=P)).then_inc(small_in, 16)
            for t_sb, t_dram in ((wv_sb, w_v), (wk_sb, w_k), (wqT_sb, w_q_t), (wout_sb, w_out), (wself_sb, w_self_t)):
                sp.dma_start(t_sb, t_dram.rearrange("(k p) o -> p k o", p=P)).then_inc(mix_in, 16)

            def load_type(i, h):
                sp.wait_ge(h_done, ((i - 1) * 2 + h + 1) * NT)
                sp.dma_start(wrel_raw[h][:],
                             w_rel_t[bass.ds(i * 2 + h, 1), :, :].rearrange("a (k p) o -> p (a k) o", p=P)
                             ).then_inc(wrel_in[h], 16)

            def types(i, last):
                for h in range(2):
                    for t in range(NT):
                        g = i * 2 * NT + h * NT + t
                        sp.wait_ge(h_copied, g + 1)
                        sp.dma_start(h_table[bass.ds((i * 2 + h) * NPAD + t * P, P), :],
                                     stage[:, (h * NT + t) % 4, :]).then_inc(h_stored[(h * NT + t) % 4], 16)
                    if not last:
                        load_type(i + 1, h)

            sp.wait_ge(mix_copied, 3 * KD)
            for b in range(2):
                sp.dma_start(wrel_raw[b][:], w_rel_t[b].rearrange("(k p) o -> p k o", p=P)).then_inc(wrel_in[b], 16)
            types(0, False)
            with sp.Fori(1, R // 2 - 1) as i:
                types(i, False)
            types(R // 2 - 1, True)

            def expert_load(i, b):
                e = i * 2 + b
                first = isinstance(i, int) and i == 0
                if not first:
                    end = sp.value_load(x_end_i[0:1, bass.ds(e - 2, 1)], min_val=1, max_val=XT_TILES + 1)
                    sp.wait_ge(w1_ready, e - 1)
                    sp.wait_ge(w1_used, end)
                sp.dma_start(w1_raw[b][:].rearrange("p (k f) -> p k f", k=KD),
                             w1[bass.ds(e, 1), :, :].rearrange("a (k p) f -> p (a k) f", p=P)).then_inc(w1_in[b], 16)
                if not first:
                    sp.wait_ge(w2_ready, e - 1)
                    sp.wait_ge(w2_used, end)
                sp.dma_start(b1_row[:, b, :], b1[bass.ds(e, 1), :].rearrange("a f -> (a f)").partition_broadcast(P)
                             ).then_inc(b1_in[b], 16)
                sp.dma_start(w2_raw[b][:].rearrange("p (k d) -> p k d", k=KF),
                             w2[bass.ds(e, 1), :, :].rearrange("a (k p) d -> p (a k) d", p=P)).then_inc(w2_in[b], 16)
                if not first:
                    sp.wait_ge(y_copied, end)
                sp.dma_start(b2_row[:, b, :], b2[bass.ds(e, 1), :].rearrange("a d -> (a d)").partition_broadcast(P)
                             ).then_inc(b2_in[b], 16)

            sp.wait_ge(base_added, NT)
            sp.wait_ge(agg_done, TILES)
            expert_load(0, 0)
            sp.wait_ge(x_scattered, 16 * 2 * NT)
            sp.wait_ge(xs_in[0], 16)
            expert_load(0, 1)
            sp.wait_ge(et_int, 2)
            with sp.Fori(1, NX // 2) as i:
                for b in range(2):
                    expert_load(i, b)

            for t in range(NT):
                n = P if t < NT - 1 else TAIL
                sp.wait_ge(out_ready, t + 1)
                sp.dma_start(out[t * P:t * P + n, :], x2[0:n, t, :]).then_inc(out_stored, 16)
            sp.wait_ge(out_stored, 16 * NT)

        @block.gpsimd
        def _(pool):
            g = nc.gpsimd
            g.memset(src_i[:, EJ:EC], 0).then_inc(edge_memset, 1)
            g.memset(dst_i[:, EJ:EC], 16 * P - 1).then_inc(edge_memset, 1)
            g.memset(typ_i[:, EJ:EC], 0).then_inc(edge_memset, 1)
            g.memset(x2[:, NT - 1, :], 0.0).then_inc(x_memset, 1)
            g.iota(diff[:], [[1, P]], base=0, channel_multiplier=-1,
                   allow_small_or_imprecise_dtypes=True).then_inc(pool_step, 1)
            g.memset(ones[:], 1.0).then_inc(consts, 1)
            pool.wait_ge(pool_step, 1)
            g.tensor_scalar(ident[:], diff[:], 0.0, None, ALU.is_equal).then_inc(consts, 1)
            g.tensor_scalar(below[:], diff[:], 0.0, None, ALU.is_gt).then_inc(consts, 1)
            g.iota(iota_h[:], [[1, TILES]], base=0, channel_multiplier=0,
                   allow_small_or_imprecise_dtypes=True).then_inc(consts, 1)
            g.iota(iota_f[:], [[1, P + 1]], base=0, channel_multiplier=0,
                   allow_small_or_imprecise_dtypes=True).then_inc(consts, 1)
            g.iota(tilecol[:], [[P, 4]], base=0, channel_multiplier=1,
                   allow_small_or_imprecise_dtypes=True).then_inc(consts, 1)
            g.memset(zeros_h[:], 0.0).then_inc(consts, 1)
            g.memset(slot_f[:], NO_TILE).then_inc(consts, 1)
            g.memset(mbd, 0.0).then_inc(consts, 1)
            g.memset(zrow, 0.0).then_inc(consts, 1)
            g.iota(order[:], [[0, NT], [-1, NX]], base=NX, channel_multiplier=0,
                   allow_small_or_imprecise_dtypes=True).then_inc(consts, 1)
            g.iota(valid[:], [[P, NT], [0, NX]], base=0, channel_multiplier=1,
                   allow_small_or_imprecise_dtypes=True).then_inc(pool_step, 1)
            pool.wait_ge(pool_step, 2)
            g.tensor_scalar(valid[:], valid[:], float(N), None, ALU.is_lt).then_inc(consts, 1)
            pool.wait_ge(consts, 12)
            pool.wait_ge(mix_in, 16 * 5)
            pool.dma_start(x_slots.rearrange("(t p) d -> p t d", p=P),
                           zrow.unsqueeze(1).to_broadcast([P, XT_TILES, D])).then_inc(x_zeroed, 16)

            def split_type(i, h):
                r = i * 2 + h
                pool.wait_ge(wrel_in[h], 16 * (i + 1))
                pool.sem_inc(split_turn, 1)
                g.tensor_scalar(wrel_hi[h][:], wrel_raw[h][:], 1.0, 0.0, ALU.mult, ALU.add).then_inc(wrel_rounded, 1)
                pool.wait_ge(wrel_rounded, r + 1)
                g.tensor_tensor(wrel_lo[h][:], wrel_raw[h][:], wrel_hi[h][:].bitcast(F32), ALU.subtract).then_inc(wrel_ready, 1)

            pool.wait_ge(bias_ready, 1)
            pool.wait_ge(xn_ready, NT)
            for t in range(NT):
                g.tensor_tensor(x2[:, t, :], x2[:, t, :], bias_row[:, 0, :], ALU.add).then_inc(x_biased, 1)
            for c in range(2):
                part_cols = slice(c * NPAD // 2, (c + 1) * NPAD // 2)
                pool.wait_ge(xnT_raw_in, (c + 1) * NT // 2)
                g.tensor_tensor(xnT_lo[:, :, part_cols], xnT_raw[:, :, part_cols], xnT_hi[:, :, part_cols].bitcast(F32),
                                ALU.subtract).then_inc(xnT_ready, 1)
            pool.wait_ge(mix_copied, 3 * KD)
            split_type(0, 0)
            for k in range(KD):
                pool.wait_ge(mix_copied, 4 * KD + k + 1)
                if k == 0:
                    pool.wait_ge(mix_in, 16 * 5)
                g.tensor_tensor(wtot[:, k, :], wtot[:, k, :], wself_sb[:, k, :], ALU.add).then_inc(wtot_ready, 1)
            pool.wait_ge(wtot_ready, KD)
            g.tensor_scalar(wtot_hi[:], wtot, 1.0, 0.0, ALU.mult, ALU.add).then_inc(wtot_rounded, 1)
            pool.wait_ge(wtot_rounded, 1)
            g.tensor_tensor(wtot_lo[:], wtot, wtot_hi[:].bitcast(F32), ALU.subtract).then_inc(wtot_split, 1)
            split_type(0, 1)
            pool.wait_ge(x_biased, NT)
            for t in range(NT):
                pool.wait_ge(base_copied, t + 1)
                g.tensor_tensor(x2[:, t, :], x2[:, t, :], base_ring[:, t % 4, :], ALU.add).then_inc(base_added, 1)
            with pool.Fori(1, R // 2) as i:
                for h in range(2):
                    split_type(i, h)

            pool.wait_ge(gidx_ready, 1)
            for n in range(4):
                pool.wait_ge(h_stored[n], 16 * (R * NT // 4))

            def gather(i):
                for h in range(2):
                    first = isinstance(i, int) and i == 0
                    pool.wait_ge(idx_copied, i * 2 + h + 1)
                    pool.sem_inc(gather_turn, 1)
                    for k in range(HALF):
                        if not (first and h == 0):
                            pool.wait_ge(agg_done, i * GRP + (h - 1) * HALF + k + 1)
                            pool.sem_inc(gather_turn, 1)
                        g.indirect_dma_start(msg[:, k, :], None, h_table,
                                             bass.IndirectOffsetOnAxis(ap=idx_ring[:, h, k:k + 1], axis=0)
                                             ).then_inc(gathered[k], 16)

            gather(0)
            with pool.Fori(1, TILES // GRP) as i:
                gather(i)

            def split(i, b):
                e = i * 2 + b
                for w_in, raw, hi, lo, rounded, ready in ((w1_in, w1_raw[b], w1_hi, w1_lo, w1_rounded, w1_ready),
                                                          (w2_in, w2_raw[b], w2_hi, w2_lo, w2_rounded, w2_ready)):
                    pool.wait_ge(w_in[b], 16 * (i + 1))
                    pool.sem_inc(split_turn, 1)
                    g.tensor_scalar(hi[:, 4 * b], raw[:], 1.0, 0.0, ALU.mult, ALU.add).then_inc(rounded, 1)
                    pool.wait_ge(rounded, e + 1)
                    pool.wait_ge((b1_in if w_in is w1_in else b2_in)[b], 16 * (i + 1))
                    g.tensor_tensor(lo[:, 4 * b], raw[:], hi[:, 4 * b].bitcast(F32), ALU.subtract).then_inc(ready, 1)

            split(0, 0)

            pool.wait_ge(slots_ready, 1)
            pool.wait_ge(xn_ready, 2 * NT)
            pool.wait_ge(x_zeroed, 16)
            for t in range(NT):
                n = P if t < NT - 1 else TAIL
                for c in range(TOPK):
                    g.indirect_dma_start(x_slots, bass.IndirectOffsetOnAxis(ap=slots_i[0:n, c, t:t + 1], axis=0),
                                         xn[0:n, t, :], None).then_inc(x_scattered, 16)
            split(0, 1)
            with pool.Fori(1, NX // 2) as i:
                for b in range(2):
                    split(i, b)
            tiles_of = [(XT_TILES + 1) // 2, XT_TILES // 2]
            for b in range(2):
                pool.wait_ge(y_stored[b], 16 * tiles_of[b])
            for t in range(NT):
                n = P if t < NT - 1 else TAIL
                for c in range(TOPK):
                    q = (t * TOPK + c) % BACK
                    if t >= BACK // TOPK:
                        pool.wait_ge(out_ready, t - BACK // TOPK + 1)
                    g.indirect_dma_start(y_ring[0:n, q, :], None, y_slots,
                                         bass.IndirectOffsetOnAxis(ap=slots_i[0:n, c, t:t + 1], axis=0)
                                         ).then_inc(y_back[q], 16)

        @block.scalar
        def _(act):
            s = nc.scalar
            square_roots(act, 0)

            def copy_h(i, h, t):
                n = h * NT + t
                act.wait_ge(h_done, i * 2 * NT + n + 1)
                if isinstance(i, int):
                    at_least(act, h_stored[n % 4], 16 * (i * 2 * NT // 4 + n // 4))
                else:
                    act.wait_ge(h_stored[n % 4], 16 * (i * (2 * NT // 4) + n // 4))
                s.copy(stage[:, n % 4, :], bank[2 + n % 2][:]).then_inc(h_copied, 1)

            n = 0
            for k in range(KD):
                n += 1
                act.wait_ge(mix_done, n)
                s.copy(gram[:, k, k * P:D], bank[n % 2][:, 0:D - k * P]).then_inc(mix_copied, 1)
            for t in range(NT):
                act.wait_ge(tr_done, t + 1)
                cols_t = slice(t * P, (t + 1) * P)
                s.copy(xnT_hi[:, :, cols_t], bank[6 + t % 2][:].rearrange("p (k m) -> p k m", k=KD))
                s.copy(xnT_raw[:, :, cols_t], bank[6 + t % 2][:].rearrange("p (k m) -> p k m", k=KD)).then_inc(xnT_raw_in, 1)
            for j in range(1, KD):
                act.wait_ge(low_done, j)
                s.copy(gram[:, j, 0:j * P], low(j)).then_inc(low_copied, 1)
            for k in range(KD):
                n += 1
                act.wait_ge(mix_done, n)
                s.copy(u_sb[:, k, :], bank[n % 2][:]).then_inc(mix_copied, 1)
            act.wait_ge(consts, 12)
            for k in range(KD):
                n += 1
                act.wait_ge(mix_done, n)
                for q in range(2):
                    c = s.mul(mbd[q * HEAD:(q + 1) * HEAD, k, q * HEAD:(q + 1) * HEAD],
                              bank[n % 2][q * HEAD:(q + 1) * HEAD, q * HEAD:(q + 1) * HEAD], MIX_SCALE)
                c.then_inc(mix_copied, 1)
            for k in range(KD):
                n += 1
                act.wait_ge(mix_done, n)
                s.copy(tt_sb[:, k, :], bank[n % 2][:]).then_inc(mix_copied, 1)
            for k in range(KD):
                n += 1
                act.wait_ge(mix_done, n)
                s.copy(wtot[:, k, :], bank[n % 2][:]).then_inc(mix_copied, 1)
            for t in range(NT):
                copy_h(0, 0, t)
            act.wait_ge(wtot_ready, KD)
            for t in range(NT):
                act.wait_ge(base_done, t + 1)
                at_least(act, base_added, t - 3)
                s.copy(base_ring[:, t % 4, :], bank[t % 2][:]).then_inc(base_copied, 1)
            for t in range(NT):
                copy_h(0, 1, t)

            def local_one_hot(j, k):
                if isinstance(j, int) and j == 0:
                    act.wait_ge(oh_ready, 1)
                if not (isinstance(j, int) and j < SORT):
                    act.wait_ge(oh_used, j - SORT + 1)
                at_least(act, loc_ready, j - 1)
                s.activation(dist[:, k % 2, :], iota_f[:, 0:P], ACT.Square, scale=-1.0,
                             bias=dloc_f[:, bass.ds(j, 1)]).then_inc(loc_dist, 1)
                act.wait_ge(loc_dist, j + 1)
                s.activation(oh_loc[:, k, :], dist[:, k % 2, :], ACT.Relu, scale=-1.0,
                             bias=ones[:, 0:1]).then_inc(loc_ready, 1)

            def copy_h_and_sort(i):
                for h in range(2):
                    for t in range(NT):
                        for j, k in columns_after(i, h * NT + t):
                            local_one_hot(j, k)
                        copy_h(i, h, t)

            copy_h_and_sort(1)
            with act.Fori(2, R // 2) as i:
                copy_h_and_sort(i)
            for j, k in LAST_COLUMNS:
                local_one_hot(j, k)

            def dst_one_hots(i):
                for n in range(GRP):
                    t = i * GRP + n
                    if n % HALF == 0:
                        if not (isinstance(i, int) and i == 0):
                            act.wait_ge(agg_done, t - HALF)
                        s.copy(idx_ring[:, n // HALF, :], gidx[:, bass.ds(t, HALF)]).then_inc(idx_copied, 1)
                    if not (isinstance(i, int) and i == 0):
                        act.wait_ge(agg_done, t - GRP + 1)
                    s.activation(dist[:, n % 2, :], iota_f[:, 1:P + 1], ACT.Square,
                                 bias=ndst[:, bass.ds(t, 1)]).then_inc(dist_ready, 1)
                    act.wait_ge(dist_ready, t + 1)
                    s.activation(oh_dst[:, n, :], dist[:, n % 2, :], ACT.Relu, scale=-1.0,
                                 bias=ones[:, 0:1]).then_inc(ohd_ready, 1)

            act.wait_ge(ndst_ready, 1)
            dst_one_hots(0)
            with act.Fori(1, TILES // GRP) as i:
                dst_one_hots(i)

            square_roots(act, 1)
            for t in range(NT):
                act.wait_ge(tr_done, NT + t + 1)
                s.copy(xnT_hi[:, :, t * P:(t + 1) * P],
                       bank[t % 2][:].rearrange("p (k m) -> p k m", k=KD)).then_inc(tr_rounded, 1)
                for c, chunk in enumerate(LOGIT_CHUNKS):
                    if t == LOGITS_AFTER[c]:
                        rows = slice(chunk[0] * P, (chunk[-1] + 1) * P)
                        act.wait_ge(lt_done, c + 1)
                        s.copy(logit_t[:, rows], bank[2 + c % 2][0:NX, 0:len(chunk) * P]).then_inc(lt_copied, 1)
            act.wait_ge(gap_ready, 1)
            s.activation(wexp[:, 1, :], wexp[:, 0, :], ACT.Exp).then_inc(exp_ready, 1)

            def load_rows(sl, b):
                act.dma_start(xs[:, b, :], x_slots[bass.ds(sl * P, P), :]).then_inc(xs_in[b], 16)

            def round_rows(sl):
                act.wait_ge(xT_done, sl + 1)
                s.copy(xT_hi[:], bank[0][:].rearrange("p (k m) -> p k m", k=KD)).then_inc(x_hi, 1)

            def expert(sl, b):
                for c in range(2):
                    act.wait_ge(hT_done, sl * 2 + c + 1)
                    s.activation(hT_hi[:, c * 4:(c + 1) * 4, :], bank[4 + c][:].rearrange("p (f m) -> p f m", m=P),
                                 ACT.Relu).then_inc(h_hi, 1)
                    if c == 0 and not (isinstance(sl, int) and sl + 1 == XT_TILES):
                        round_rows(sl + 1)
                        if not (isinstance(sl, int) and sl + 3 >= XT_TILES):
                            load_rows(sl + 3, 1 - b)
                act.wait_ge(y_copied, sl + 2)
                act.dma_start(y_slots[bass.ds(sl * P, P), :], y_sb[:, b, :]).then_inc(y_stored[b], 16)

            act.wait_ge(x_scattered, 16 * 2 * NT)
            load_rows(0, 0)
            load_rows(1, 1)
            round_rows(0)
            load_rows(2, 0)
            expert(0, 0)
            expert(1, 1)
            with act.Fori(1, (XT_TILES - 3) // 2) as i:
                for b in range(2):
                    expert(i * 2 + b, b)
            for sl in range(XT_TILES - 3, XT_TILES):
                expert(sl, sl % 2)

        @block.tensor
        def _(pe):
            mm = nc.tensor.matmul

            def three(psum, l_hi, l_lo, w_hi, w_lo, start, stop):
                mm(psum, l_hi, w_hi, start=start, stop=False)
                mm(psum, l_lo, w_hi, start=False, stop=False)
                return mm(psum, l_hi, w_lo, start=False, stop=stop)

            def transpose_rows(t, m):
                for k in range(KD):
                    last = nc.tensor.transpose(bank[m][:, k * P:(k + 1) * P], xn[:, t, k * P:(k + 1) * P], ident[:])
                last.then_inc(tr_done, 1)

            def h_tile(i, h, t):
                n = h * NT + t
                if t == 0:
                    pe.wait_ge(wrel_ready, i * 2 + h + 1)
                if not (isinstance(i, int) and i * 2 * NT + n < 2):
                    pe.wait_ge(h_copied, i * 2 * NT + n - 1)
                for k in range(KD):
                    rows = slice(t * P, (t + 1) * P)
                    last = three(bank[2 + n % 2][:], xnT_hi[:, k, rows], xnT_lo[:, k, rows],
                                 wrel_hi[h][:, k, :], wrel_lo[h][:, k, :], k == 0, k == KD - 1)
                last.then_inc(h_done, 1)

            pe.wait_ge(consts, 12)
            n = 0

            def small(m, k_range, lhs, rhs, done, width=D):
                for j, k in enumerate(k_range):
                    if m == 1:
                        pe.wait_ge(xn_ready, k + 1)
                    last = mm(bank[m % 2][:, 0:width], lhs(k), rhs(k), start=(j == 0), stop=(j == len(k_range) - 1))
                last.then_inc(done, 1)

            for k in range(KD):
                n += 1
                at_least(pe, mix_copied, n - 2)
                small(n, range(NT), lambda t: xn[:, t, k * P:(k + 1) * P], lambda t: xn[:, t, k * P:D], mix_done, D - k * P)
            pe.wait_ge(mix_copied, n)
            for t in range(NT):
                at_least(pe, xnT_raw_in, t - 1)
                transpose_rows(t, 6 + t % 2)
            pe.wait_ge(mix_in, 16 * 5)
            for j in range(1, KD):
                pe.wait_ge(mix_copied, j)
                for k in range(j):
                    last = nc.tensor.transpose(low(j)[:, k * P:(k + 1) * P], gram[:, k, j * P:(j + 1) * P], ident[:])
                last.then_inc(low_done, 1)
            pe.wait_ge(mix_copied, n)
            pe.wait_ge(low_copied, KD - 1)
            for k in range(KD):
                n += 1
                at_least(pe, mix_copied, n - 2)
                if k == KD - 1:
                    pe.wait_ge(tot_ready, NB)
                    mm(bank[4][:, 0:NB], below[:], tot[:], start=True, stop=True)
                    mm(bank[4][:, NB:2 * NB], ones[:], tot[:], start=True, stop=True).then_inc(off_done, 1)
                small(n, range(KD), lambda j: gram[:, j, k * P:(k + 1) * P], lambda j: wv_sb[:, j, :], mix_done)
            pe.wait_ge(mix_copied, n)
            for k in range(KD):
                n += 1
                at_least(pe, mix_copied, n - 2)
                small(n, range(KD), lambda j: wk_sb[:, j, k * P:(k + 1) * P],
                      lambda j: u_sb[:, j, k * P:(k + 1) * P], mix_done, P)
            pe.wait_ge(mix_copied, n)
            for k in range(KD):
                n += 1
                at_least(pe, mix_copied, n - 2)
                small(n, [k], lambda j: mbd[:, j, :], lambda j: wqT_sb[:, j, :], mix_done)
            pe.wait_ge(mix_copied, n)
            for k in range(KD):
                n += 1
                pe.wait_ge(mix_copied, n - 2)
                small(n, range(KD), lambda j: tt_sb[:, j, k * P:(k + 1) * P], lambda j: wout_sb[:, j, :], mix_done)

            for t in range(NT):
                if t % (NT // 2) == 0:
                    pe.wait_ge(xnT_ready, t // (NT // 2) + 1)
                h_tile(0, 0, t)
            pe.wait_ge(bt_ready, 1)
            for m in range(4):
                last = mm(bank[4][0:1, m * P:(m + 1) * P], bt_col[:, m:m + 1], ident[:], start=True, stop=True)
            last.then_inc(bt_done, 1)
            pe.wait_ge(wtot_split, 1)
            for t in range(NT):
                at_least(pe, base_copied, t - 1)
                rows = slice(t * P, (t + 1) * P)
                for k in range(KD):
                    last = three(bank[t % 2][:], xnT_hi[:, k, rows], xnT_lo[:, k, rows], wtot_hi[:, k, :], wtot_lo[:, k, :],
                                 k == 0, k == KD - 1)
                last.then_inc(base_done, 1)
            for t in range(NT):
                h_tile(0, 1, t)

            def sort_column(j, k, start=False, stop=False):
                pe.wait_ge(oh_ready, j + 1)
                mm(bank[5][:, 0:TILES], row_src[:, k, :], oh_tile[:, k, :], start=start, stop=stop, skip_group_check=True)
                mm(bank[6][:, 0:TILES], row_code[:, k, :], oh_tile[:, k, :], start=start, stop=stop, skip_group_check=True)
                pe.wait_ge(loc_ready, j + 1)
                mm(bank[7][:, 0:NB], oh_loc[:, k, :], oh_bkt[:, k, :], start=start, stop=stop,
                   skip_group_check=True).then_inc(oh_used, 1)

            def types_and_sort(i):
                for h in range(2):
                    for t in range(NT):
                        h_tile(i, h, t)
                        for j, k in columns_after(i, h * NT + t):
                            sort_column(j, k, start=(isinstance(j, int) and j == 0))

            types_and_sort(1)
            with pe.Fori(2, R // 2) as i:
                types_and_sort(i)
            for j, k in LAST_COLUMNS:
                sort_column(j, k, stop=(j == EC - 1))

            def aggregate(i):
                for h in range(2):
                    for k in range(HALF):
                        first = isinstance(i, int) and i == 0 and h == 0
                        t = i * GRP + h * HALF + k
                        pe.wait_ge(gathered[k], 16 * (i * 2 + h + 1))
                        pe.wait_ge(ohd_ready, t + 1)
                        if not first:
                            pe.wait_ge(agg_added, 2 * (t - HALF + 1))
                        mm(bank[k][:], oh_dst[:, h * HALF + k, :], msg[:, k, :], start=True, stop=True).then_inc(agg_done, 1)

            pe.wait_ge(gidx_ready, 1)
            aggregate(0)
            with pe.Fori(1, TILES // GRP) as i:
                aggregate(i)

            pe.wait_ge(gate_ready, 1)
            def logits(c):
                tiles = LOGIT_CHUNKS[c]
                rows = slice(tiles[0] * P, (tiles[-1] + 1) * P)
                pe.wait_ge(tr_copied, tiles[-1] + 1)
                at_least(pe, lt_copied, c - 1)
                for k in range(KD):
                    last = three(bank[2 + c % 2][0:NX, 0:len(tiles) * P], gate_hi[:, k, :], gate_lo[:, k, :],
                                 xnT_hi[:, k, rows], xnT_lo[:, k, rows], k == 0, k == KD - 1)
                last.then_inc(lt_done, 1)

            def transpose_logits(c):
                pe.wait_ge(lt_copied, c + 1)
                for t in LOGIT_CHUNKS[c]:
                    last = nc.tensor.transpose(bank[5][:, t * NX:(t + 1) * NX], logit_t[:, t * P:(t + 1) * P],
                                               ident[0:NX, 0:NX])
                return last

            for t in range(NT):
                pe.wait_ge(xn_ready, NT + t + 1)
                at_least(pe, tr_copied, t - 1)
                transpose_rows(t, t % 2)
                for c in range(len(LOGIT_CHUNKS)):
                    if t == LOGITS_AFTER[c]:
                        logits(c)
            for c in range(len(LOGIT_CHUNKS)):
                last = transpose_logits(c)
            last.then_inc(logit_done, 1)
            pe.wait_ge(took_ready, 1)
            mm(bank[3][:, 0:NX * NT], below[:], took[:].rearrange("p e t -> p (e t)"), start=True, stop=True)
            mm(bank[3][:, NX * NT:2 * NX * NT], ones[:], took[:].rearrange("p e t -> p (e t)"),
               start=True, stop=True).then_inc(cum_done, 1)
            pe.wait_ge(et_ready, 1)
            mm(bank[4][0:1, 0:P], et_col[:], ident[:], start=True, stop=True).then_inc(et_done, 1)
            def rows_of(b, cnt):
                pe.wait_ge(xs_in[b], 16 * cnt)
                for k in range(KD):
                    last = nc.tensor.transpose(bank[0][:, k * P:(k + 1) * P], xs[:, b, k * P:(k + 1) * P], ident[:])
                last.then_inc(xT_done, 1)

            def expert(sl, b, next_cnt, ahead):
                e = pe.value_load(et_i[0:1, bass.ds(sl, 1)], min_val=0, max_val=NX - 1)
                par = pe.snap(e % 2 * 4)
                need = pe.snap(e + 1)

                def first(c, ks):
                    for k in ks:
                        cols = slice(k * F + c * D, k * F + (c + 1) * D)
                        last = three(bank[2 + c][:], xT_hi[:, k, :], xT_lo[:, k, :],
                                     w1_hi[:, bass.ds(par, 1), cols], w1_lo[:, bass.ds(par, 1), cols],
                                     k == 0, k == KD - 1)
                    return last

                def second(fs):
                    for f in fs:
                        cols = slice(f * D, (f + 1) * D)
                        last = three(bank[6 + b][:], hT_hi[:, f, :], hT_lo[:, f, :],
                                     w2_hi[:, bass.ds(par, 1), cols], w2_lo[:, bass.ds(par, 1), cols],
                                     f == 0, f == KF - 1)
                    return last

                def transpose_hidden(c):
                    pe.wait_ge(hid_ready, sl * 2 + c + 1)
                    for f in range(4):
                        last = nc.tensor.transpose(bank[4 + c][:, f * P:(f + 1) * P],
                                                   hid[:, (c * 4 + f) * P:(c * 4 + f + 1) * P], ident[:])
                    last.then_inc(hT_done, 1)

                pe.wait_ge(x_lo, sl + 1)
                pe.wait_ge(w1_ready, need)
                first(0, range(KD)).then_inc(l1_half_done, 1)
                first(1, range(KD // 2))
                transpose_hidden(0)
                first(1, range(KD // 2, KD)).then_inc(w1_used, 1)
                if ahead:
                    rows_of(1 - b, next_cnt)
                pe.wait_ge(w2_ready, need)
                pe.wait_ge(h_lo, sl * 2 + 1)
                if not (isinstance(sl, int) and sl < 2):
                    pe.wait_ge(y_copied, sl)
                second(range(0, 2))
                transpose_hidden(1)
                second(range(2, 4))
                pe.wait_ge(h_lo, sl * 2 + 2)
                second(range(4, KF)).then_inc(w2_used, 1)

            pe.wait_ge(et_int, 2)
            pe.sem_inc(w1_used, 1)
            pe.sem_inc(w2_used, 1)
            rows_of(0, 1)
            expert(0, 0, 1, True)
            expert(1, 1, 2, True)
            with pe.Fori(1, (XT_TILES - 3) // 2) as i:
                expert(i * 2, 0, i + 1, True)
                expert(i * 2 + 1, 1, i + 2, True)
            for sl in range(XT_TILES - 3, XT_TILES):
                expert(sl, sl % 2, (sl + 1) // 2 + 1, sl + 1 < XT_TILES)

        @block.vector
        def _(dve):
            v = nc.vector
            steps = [0]

            def link(ins):
                steps[0] += 1
                ins.then_inc(dve_step, 1)
                dve.wait_ge(dve_step, steps[0])

            def layer_norm(rnd):
                for h, tiles in enumerate(HALVES):
                    for t in tiles:
                        if rnd == 0 and t in (tiles[0], NT - 1):
                            dve.wait_ge(x_in[h] if t < NT - 1 else x_tail_in, 16)
                        last = v.bn_stats(stats[:, t, :], x2[:, t, :])
                    link(last)
                    for t in tiles:
                        last = v.bn_aggr(mv[:, t, :], stats[:, t, :])
                    link(last)
                    part = slice(tiles[0], tiles[-1] + 1)
                    v.tensor_scalar(vare[:, part], mv[:, part, 1], EPS, None, ALU.add).then_inc(var_ready, 1)
                    dve.wait_ge(std_ready, 2 * rnd + h + 1)
                    link(v.reciprocal(rstd[:, part], std[:, part]))
                    for t in tiles:
                        v.tensor_scalar(xn[:, t, :], x2[:, t, :], mv[:, t, 0:1], rstd[:, t:t + 1],
                                        ALU.subtract, ALU.mult).then_inc(xn_ready, 1)

            dve.wait_ge(edges_in, 16 * 6)
            dve.wait_ge(edge_memset, 3)
            link(v.tensor_scalar(tmp_i[:], dst_i[:], P - 1, None, ALU.bitwise_and))
            v.tensor_copy(src_f[:], src_i[:])
            link(v.tensor_copy(dloc_f[:], tmp_i[:]))
            link(v.scalar_tensor_tensor(code_f[:], typ_i[:], float(P), dloc_f[:], ALU.mult, ALU.add))
            link(v.tensor_scalar(code_f[:], code_f[:], 1024.0, None, ALU.add))
            link(v.tensor_scalar(tmp_i[:], dst_i[:], 7, None, ALU.arith_shift_right))
            link(v.scalar_tensor_tensor(bkt_f[:], tmp_i[:], float(R), typ_i[:], ALU.mult, ALU.add))
            link(v.tensor_copy(bkt_h[:], bkt_f[:]))

            layer_norm(0)

            dve.wait_ge(small_in, 16 * 4)
            v.tensor_tensor(bias_row[:, 0, :], bias_row[:, 0, :], bias_row[:, 1, :], ALU.add).then_inc(bias_ready, 1)
            v.tensor_copy(gate_hi[:], gate_sb[:]).then_inc(gate_rounded, 1)
            dve.wait_ge(gate_rounded, 1)
            v.tensor_tensor(gate_lo[:], gate_sb[:], gate_hi[:].bitcast(F32), ALU.subtract).then_inc(gate_ready, 1)

            dve.wait_ge(consts, 12)
            def count_buckets(i):
                for q in range(2):
                    b = i * 2 + q
                    at_least(dve, tot_ready, b - 1)
                    v.tensor_scalar(eq_h[:, q, :], bkt_h[:], iota_f[:, bass.ds(b, 1)], None, ALU.is_equal,
                                    ALU.add, accum_out=tot[:, bass.ds(b, 1)]).then_inc(tot_ready, 1)

            count_buckets(0)
            with dve.Fori(1, NB // 2) as i:
                count_buckets(i)

            dve.wait_ge(off_done, 1)
            n_tiles, end_tile, start_tile, from_0 = (cols[:, n, :] for n in range(4))
            link(v.tensor_scalar(cols_i[:, 0, :], bank[4][:, NB:2 * NB], float(P - 1), None, ALU.add))
            link(v.tensor_scalar(cols_i[:, 1, :], cols_i[:, 0, :], 7, None, ALU.arith_shift_right))
            link(v.tensor_copy(n_tiles, cols_i[:, 1, :]))
            link(v.tensor_tensor_scan(end_tile, n_tiles, zeros_h[:, 0:NB], 0.0, ALU.add, ALU.add))
            link(v.tensor_tensor(start_tile, end_tile, n_tiles, ALU.subtract))
            link(v.scalar_tensor_tensor(from_0, start_tile, float(P), bank[4][:, 0:NB], ALU.mult, ALU.add))
            link(v.tensor_scalar(rank_from[:], from_0, -1.0, None, ALU.add))
            for m in range(4):
                last = v.tensor_scalar(bt_junk[:, m, :], end_tile, tilecol[:, m:m + 1], None, ALU.is_le, ALU.add,
                                       accum_out=bt_col[:, m:m + 1])
            last.then_inc(bt_ready, 1)

            def rank_buckets(i):
                for q in range(2):
                    b = i * 2 + q
                    at_least(dve, slots_set, b - 1)
                    v.tensor_scalar(eq_h[:, q, :], bkt_h[:], iota_f[:, bass.ds(b, 1)], None, ALU.is_equal).then_inc(rank1, 1)
                for q in range(2):
                    b = i * 2 + q
                    dve.wait_ge(rank1, b + 1)
                    v.tensor_tensor_scan(rank_f[:, q, :], eq_h[:, q, :], zeros_h[:], rank_from[:, bass.ds(b, 1)],
                                         ALU.add, ALU.add).then_inc(rank2, 1)
                for q in range(2):
                    b = i * 2 + q
                    at_least(dve, slots_set, b)
                    dve.wait_ge(rank2, b + 1)
                    dve.sem_inc(copy_turn, 1)
                    v.copy_predicated(slot_f[:], eq_h[:, q, :].bitcast(mybir.dt.int16), rank_f[:, q, :]).then_inc(slots_set, 1)

            dve.wait_ge(tot_ready, NB)
            rank_buckets(0)
            with dve.Fori(1, NB // 2) as i:
                rank_buckets(i)
            dve.wait_ge(slots_set, NB)
            link(v.tensor_copy(slot_i[:], slot_f[:]))
            link(v.tensor_scalar(tmp_i[:], slot_i[:], P - 1, None, ALU.bitwise_and))
            link(v.tensor_copy(row_f, tmp_i[:]))
            link(v.tensor_scalar(tmp_i[:], slot_i[:], 7, None, ALU.arith_shift_right))
            link(v.tensor_copy(tile_f, tmp_i[:]))

            dve.wait_ge(bt_done, 1)
            link(v.tensor_scalar(bt_f[:], bank[4][0:1, :], float(NB - 1), None, ALU.min))
            two = bt_f[:].rearrange("p (m a) -> p m a", a=2)
            link(v.scalar_tensor_tensor(bt_pair[:], two[:, :, 1], float(NB), two[:, :, 0], ALU.mult, ALU.add))

            def one_hots(j, k):
                if not (isinstance(j, int) and j < SORT):
                    dve.wait_ge(oh_used, j - SORT + 1)
                row, tile = row_f[:, bass.ds(j, 1)], tile_f[:, bass.ds(j, 1)]
                v.tensor_scalar(row_src[:, k, :], iota_h[:, 0:P], row, src_f[:, bass.ds(j, 1)], ALU.is_equal, ALU.mult)
                v.tensor_scalar(row_code[:, k, :], iota_h[:, 0:P], row, code_f[:, bass.ds(j, 1)], ALU.is_equal, ALU.mult)
                v.tensor_scalar(oh_bkt[:, k, :], iota_h[:, 0:NB], bkt_f[:, bass.ds(j, 1)], None, ALU.is_equal)
                v.tensor_scalar(oh_tile[:, k, :], iota_h[:], tile, None, ALU.is_equal).then_inc(oh_ready, 1)

            for k in range(SORT):
                one_hots(k, k)
            with dve.Fori(1, EC // SORT) as i:
                for k in range(SORT):
                    one_hots(i * SORT + k, k)
            for j, k in LAST_COLUMNS:
                one_hots(j, k)

            dve.wait_ge(oh_used, EC)
            link(v.tensor_scalar(inv_cnt[:], bank[7][:, 0:NB], 1.0, None, ALU.max))
            link(v.reciprocal(inv_cnt[:], inv_cnt[:]))
            link(v.tensor_copy(code_i, bank[6][:, 0:TILES]))
            link(v.tensor_scalar(part_i[:, 0, :], code_i, 7, R - 1, ALU.arith_shift_right, ALU.bitwise_and))
            v.scalar_tensor_tensor(gidx[:], part_i[:, 0, :], float(NPAD), bank[5][:, 0:TILES], ALU.mult, ALU.add).then_inc(gidx_ready, 1)
            dve.wait_ge(gidx_ready, 1)
            v.tensor_scalar(part_i[:, 0, :], code_i, P - 1, None, ALU.bitwise_and)
            link(v.tensor_scalar(part_i[:, 1, :], code_i, 10, None, ALU.arith_shift_right))
            v.scalar_tensor_tensor(ndst[:], part_i[:, 1, :], -1.0, part_i[:, 0, :], ALU.mult, ALU.subtract).then_inc(ndst_ready, 1)

            def add_messages(i):
                _, pairs = nc.values_load_multi_w_load_instructions(
                    bt_pair[0:1, bass.ds(i * HALF, HALF)], engines=[mybir.EngineType.DVE], min_val=0,
                    max_val=NB * NB - 1)
                for n in range(GRP):
                    t = i * GRP + n
                    bucket = dve.snap(pairs[n // 2] // NB if n % 2 else pairs[n // 2] % NB)
                    row = dve.snap(bucket // R * D)
                    for h in range(2):
                        if h == 0:
                            dve.wait_ge(agg_done, t + 1)
                        at_least(dve, agg_added, 2 * t + h - 1)
                        into = x2_flat[:, bass.ds(row + h * (D // 2), D // 2)]
                        v.scalar_tensor_tensor(into, bank[n % HALF][:, h * (D // 2):(h + 1) * (D // 2)],
                                               inv_cnt[:, bass.ds(bucket, 1)], into, ALU.mult, ALU.add).then_inc(agg_added, 1)

            x2_flat = x2[:].rearrange("p t d -> p (t d)")
            dve.wait_ge(base_added, NT)
            add_messages(0)
            with dve.Fori(1, TILES // GRP) as i:
                add_messages(i)
            dve.wait_ge(agg_added, 2 * TILES)

            layer_norm(1)

            for t in range(NT):
                dve.wait_ge(tr_rounded, t + 1)
                rows = slice(t * P, (t + 1) * P)
                v.tensor_tensor(xnT_lo[:, :, rows], bank[t % 2][:].rearrange("p (k m) -> p k m", k=KD),
                                xnT_hi[:, :, rows].bitcast(F32), ALU.subtract).then_inc(tr_copied, 1)

            dve.wait_ge(logit_done, 1)
            link(v.tensor_tensor(logit[:], bank[5][:, 0:NT * NX].rearrange("p (t e) -> p t e", t=NT),
                                 gb_row[:].unsqueeze(1).to_broadcast([P, NT, NX]), ALU.add))
            values = logit
            for c in range(TOPK):
                link(v.tensor_reduce(top[:, c, :], values[:], AX_X, ALU.max))
                link(v.tensor_tensor(score[:], values[:], top[:, c, :].unsqueeze(2).to_broadcast([P, NT, NX]), ALU.is_equal))
                link(v.tensor_tensor(score[:], score[:], order[:], ALU.mult))
                link(v.tensor_reduce(best[:], score[:], AX_X, ALU.max))
                link(v.tensor_tensor(pick[:, c], order[:], best[:].unsqueeze(2).to_broadcast([P, NT, NX]), ALU.is_equal))
                if c == 0:
                    link(v.tensor_scalar(masked[:], pick[:, 0], -3e38, 1.5e38, ALU.mult, ALU.add))
                    link(v.tensor_tensor(masked[:], masked[:], logit[:], ALU.min))
                    values = masked
            v.tensor_tensor(wexp[:, 0, :], top[:, 1, :], top[:, 0, :], ALU.subtract).then_inc(gap_ready, 1)
            for c in range(TOPK):
                link(v.tensor_tensor(pick[:, c], pick[:, c], valid[:], ALU.mult))
            v.tensor_tensor(took[:].rearrange("p e t -> p t e"), pick[:, 0], pick[:, 1], ALU.add).then_inc(took_ready, 1)
            dve.wait_ge(exp_ready, 1)
            link(v.tensor_scalar(wexp[:, 2, :], wexp[:, 1, :], 1.0, None, ALU.add))
            link(v.reciprocal(wts[:, 0, :], wexp[:, 2, :]))
            v.tensor_tensor(wts[:, 1, :], wexp[:, 1, :], wts[:, 0, :], ALU.mult).then_inc(wts_ready, 1)
            dve.wait_ge(cum_done, 1)
            within = bank[3][:, 0:NX * NT].rearrange("p (e t) -> p e t", e=NX)
            per_tile = bank[3][:, NX * NT:2 * NX * NT].rearrange("p (e t) -> p e t", e=NX)
            x_count, x_tiles, x_end, x_from = (xcols[:, n, :] for n in range(4))
            link(v.tensor_copy(tsum[:], per_tile))
            link(v.tensor_reduce(x_count, tsum[:], AX_X, ALU.add))
            link(v.tensor_tensor_scan(tcum[:].rearrange("p e t -> p (e t)"), tsum[:].rearrange("p e t -> p (e t)"),
                                      zeros_h[:, 0:NX * NT], 0.0, ALU.add, ALU.add))
            link(v.tensor_tensor(tcum[:], tcum[:], tsum[:], ALU.subtract))
            link(v.tensor_scalar(xcols_i[:], x_count, float(P - 1), None, ALU.add))
            link(v.tensor_scalar(xcols_i[:], xcols_i[:], 7, None, ALU.arith_shift_right))
            link(v.tensor_copy(x_tiles, xcols_i[:]))
            link(v.tensor_tensor_scan(x_end, x_tiles, zeros_h[:, 0:NX], 0.0, ALU.add, ALU.add))
            link(v.tensor_scalar(et_junk[:], x_end, tilecol[:, 0:1], None, ALU.is_le, ALU.add, accum_out=et_col[:]))
            v.tensor_scalar(et_col[:], et_col[:], float(NX - 1), None, ALU.min).then_inc(et_ready, 1)
            link(v.tensor_tensor(x_from, x_end, x_tiles, ALU.subtract))
            link(v.scalar_tensor_tensor(x_from, x_from, float(P), tcum[:, :, 0], ALU.mult, ALU.subtract))
            link(v.tensor_tensor(xslot[:], tcum[:], within, ALU.add))
            link(v.tensor_tensor(xslot[:], xslot[:], x_from.unsqueeze(2).to_broadcast([P, NX, NT]), ALU.add))
            for c in range(TOPK):
                link(v.tensor_tensor(pick_slot[:], pick[:, c], xslot[:].rearrange("p e t -> p t e"), ALU.mult))
                link(v.tensor_reduce(slots_f[:, c, :], pick_slot[:], AX_X, ALU.add))
            v.tensor_copy(slots_i[:], slots_f[:]).then_inc(slots_ready, 1)
            dve.wait_ge(et_done, 1)
            v.tensor_copy(et_i[:], bank[4][0:1, 0:P]).then_inc(et_int, 1)
            v.tensor_scalar(x_end_i[:], x_end[0:1, :], 1.0, None, ALU.add).then_inc(et_int, 1)

            def rest_rows(sl):
                dve.wait_ge(x_hi, sl + 1)
                v.tensor_tensor(xT_lo[:], bank[0][:].rearrange("p (k m) -> p k m", k=KD), xT_hi[:].bitcast(F32),
                                ALU.subtract).then_inc(x_lo, 1)

            def hidden(sl, c, par):
                if c == 0:
                    dve.wait_ge(l1_half_done, sl + 1)
                else:
                    dve.wait_ge(w1_used, sl + 2)
                v.tensor_tensor(hid[:, c * D:(c + 1) * D], bank[2 + c][:],
                                b1_row[:, bass.ds(par, 1), c * D:(c + 1) * D], ALU.add).then_inc(hid_ready, 1)

            def rest_hidden(sl, c):
                dve.wait_ge(h_hi, sl * 2 + c + 1)
                v.scalar_tensor_tensor(hT_lo[:, c * 4:(c + 1) * 4, :], bank[4 + c][:].rearrange("p (f m) -> p f m", m=P), 0.0,
                                       hT_hi[:, c * 4:(c + 1) * 4, :].bitcast(F32), ALU.max, ALU.subtract).then_inc(h_lo, 1)

            def expert(sl, b, cnt):
                e = dve.value_load(et_i[0:1, bass.ds(sl, 1)], min_val=0, max_val=NX - 1)
                par = dve.snap(e % 2)
                hidden(sl, 0, par)
                rest_hidden(sl, 0)
                hidden(sl, 1, par)
                if not (isinstance(sl, int) and sl + 1 == XT_TILES):
                    rest_rows(sl + 1)
                rest_hidden(sl, 1)
                dve.wait_ge(w2_used, sl + 2)
                at_least(dve, y_stored[b], 16 * cnt)
                v.tensor_tensor(y_sb[:, b, :], bank[6 + b][:], b2_row[:, bass.ds(par, 1), :], ALU.add).then_inc(y_copied, 1)

            dve.wait_ge(et_int, 2)
            dve.sem_inc(y_copied, 1)
            rest_rows(0)
            expert(0, 0, 0)
            expert(1, 1, 0)
            with dve.Fori(1, (XT_TILES - 3) // 2) as i:
                for b in range(2):
                    expert(i * 2 + b, b, i)
            for sl in range(XT_TILES - 3, XT_TILES):
                expert(sl, sl % 2, sl // 2)

            dve.wait_ge(wts_ready, 1)
            for t in range(NT):
                for c in range(TOPK):
                    q = (t * TOPK + c) % BACK
                    n = P if t < NT - 1 else TAIL
                    dve.wait_ge(y_back[q], 16 * ((t * TOPK + c) // BACK + 1))
                    ins = v.scalar_tensor_tensor(x2[0:n, t, :], y_ring[0:n, q, :], wts[0:n, c, t:t + 1], x2[0:n, t, :],
                                                 ALU.mult, ALU.add)
                    if c == 0:
                        link(ins)
                ins.then_inc(out_ready, 1)


_INS = ["x", "src", "dst", "edge_type", "w_self_t", "w_rel_t", "gnn_bias", "w_q_t", "w_k", "w_v", "w_out", "b_out",
        "gate_w", "gate_b", "w1", "b1", "w2", "b2"]


def kernel(x, src, dst, edge_type_8, L0_gnn_W_self, L0_gnn_W_rel, L0_gnn_bias, L0_mix_w_qkv, L0_mix_w_out,
           L0_mix_b_out, L0_ffn_gate_w, L0_ffn_gate_b, L0_ffn_w1, L0_ffn_b1, L0_ffn_w2, L0_ffn_b2):
    import numpy as np
    import concourse.bacc as bacc
    from concourse.bass_utils import run_bass_kernel_spmd

    x = np.asarray(x)
    dim = x.shape[1]
    qkv = np.asarray(L0_mix_w_qkv)
    laid = dict(zip(_INS, [
        x, src, dst, edge_type_8,
        np.asarray(L0_gnn_W_self).T, np.asarray(L0_gnn_W_rel).transpose(0, 2, 1), L0_gnn_bias,
        qkv[:, 0:dim].T, qkv[:, dim:2 * dim], qkv[:, 2 * dim:3 * dim], L0_mix_w_out, L0_mix_b_out,
        L0_ffn_gate_w, L0_ffn_gate_b, L0_ffn_w1, L0_ffn_b1, L0_ffn_w2, L0_ffn_b2]))
    nc = bacc.Bacc("TRN2", target_bir_lowering=False, num_devices=1)
    arrays, args = {}, []
    for name in _INS:
        a = np.ascontiguousarray(laid[name])
        arrays[f"in_{name}"] = a
        args.append(nc.dram_tensor(f"in_{name}", a.shape, mybir.dt.from_np(a.dtype), kind="ExternalInput").ap())
    out = nc.dram_tensor("out_0", x.shape, F32, kind="ExternalOutput").ap()
    gnn_moe_kernel(nc, *args, out)
    return run_bass_kernel_spmd(nc, [arrays], core_ids=[0]).results[0]["out_0"]
```
